# Optimizing a Trainium2 kernel written in Bass

```python
import numpy as np
import jax
import jax.numpy as jnp

def _softmax(x, axis=-1):
    return jax.nn.softmax(x, axis=axis)

def _gelu(x):
    return jax.nn.gelu(x, approximate=True)

def _silu(x):
    return jax.nn.silu(x)

def _sigmoid(x):
    return jax.nn.sigmoid(x)

def _layernorm(x, axis=-1, eps=1e-05):
    m = jnp.mean(x, axis=axis, keepdims=True)
    v = jnp.var(x, axis=axis, keepdims=True)
    return (x - m) / jnp.sqrt(v + eps)

def _scatter_add(tgt, idx, src, axis=0):
    return tgt.at[idx].add(src)

def _segment_sum(src, seg, n):
    return jax.ops.segment_sum(src, seg, n)
kernel_name = 'mk_adaln_ffn_d1_seqx_r8_0ed05b'

def setup_inputs(seed: int=0):
    np.random.seed(seed)
    _w = jnp.asarray

    def _rec_inputs():
        import jax
        import jax.numpy as jnp
        _rk = jax.random.key(seed)
        x = -0.000125 + 0.9999 * jax.random.normal(jax.random.fold_in(_rk, 1), (2, 512, 128), jnp.float32)
        _lenS = 512 - jax.random.randint(jax.random.fold_in(_rk, 7), (2,), 0, max(1, 512 // 4) + 1, jnp.int32)
        _lenS2 = 512 - jax.random.randint(jax.random.fold_in(_rk, 8), (2,), 0, max(1, 512 // 4) + 1, jnp.int32)
        cond_512 = 0.0061147 + 1.02565 * jax.random.normal(jax.random.fold_in(_rk, 11), (2, 64), jnp.float32)
        return (x, cond_512)
    x, cond_512 = _rec_inputs()

    def _L0_cond_setup():
        import jax, jax.numpy as jnp
        import numpy as np
        B, S, D, H, C = (8, 512, 128, 32, 64)
        INIT_RANGE = 0.01
        key = jax.random.key(seed)
        ks = jax.random.split(key, 6)
        return {'hidden_states': jax.random.normal(ks[0], (B, S, D), dtype=jnp.float32), 'conditions': jax.random.normal(ks[1], (B, C), dtype=jnp.float32), 'down_project': jax.random.normal(ks[2], (D, H), dtype=jnp.float32) * INIT_RANGE, 'down_gamma': jax.random.normal(ks[3], (C, H), dtype=jnp.float32), 'down_beta': jnp.zeros((C, H), dtype=jnp.float32), 'up_project': jax.random.normal(ks[4], (H, D), dtype=jnp.float32) * INIT_RANGE, 'up_gamma': jax.random.normal(ks[5], (C, D), dtype=jnp.float32), 'up_beta': jnp.zeros((C, D), dtype=jnp.float32)}
    _L0_cond_all = _L0_cond_setup()
    _L0_cond_in = {k: v for k, v in _L0_cond_all.items() if k in ('down_project', 'down_gamma', 'down_beta', 'up_project', 'up_gamma', 'up_beta')}
    del _L0_cond_all

    def _L0_ffn_setup():
        import jax, jax.numpy as jnp
        import numpy as np
        B, S, D, F, E, NS, K = (2, 128, 128, 512, 8, 8, 2)
        FS = F // NS
        key = jax.random.key(seed)
        ks = jax.random.split(key, 8)
        scale = 0.02
        return {'hidden_states': jax.random.normal(ks[0], (B, S, D), jnp.float32), 'gate_W': jax.random.normal(ks[1], (E, D), jnp.float32) * scale, 'w1_e': jax.random.normal(ks[2], (E, D, F), jnp.float32) * scale, 'w3_e': jax.random.normal(ks[3], (E, D, F), jnp.float32) * scale, 'w2_e': jax.random.normal(ks[4], (E, F, D), jnp.float32) * scale, 'w1_s': jax.random.normal(ks[5], (NS, D, FS), jnp.float32) * scale, 'w3_s': jax.random.normal(ks[6], (NS, D, FS), jnp.float32) * scale, 'w2_s': jax.random.normal(ks[7], (NS, FS, D), jnp.float32) * scale}
    _L0_ffn_all = _L0_ffn_setup()
    _L0_ffn_in = {k: v for k, v in _L0_ffn_all.items() if k in ('gate_W', 'w1_e', 'w3_e', 'w2_e', 'w1_s', 'w3_s', 'w2_s')}
    del _L0_ffn_all
    return {'x': x, 'cond_512': cond_512, 'L0_cond_down_project': _L0_cond_in['down_project'], 'L0_cond_down_gamma': _L0_cond_in['down_gamma'], 'L0_cond_down_beta': _L0_cond_in['down_beta'], 'L0_cond_up_project': _L0_cond_in['up_project'], 'L0_cond_up_gamma': _L0_cond_in['up_gamma'], 'L0_cond_up_beta': _L0_cond_in['up_beta'], 'L0_ffn_gate_W': _L0_ffn_in['gate_W'], 'L0_ffn_w1_e': _L0_ffn_in['w1_e'], 'L0_ffn_w3_e': _L0_ffn_in['w3_e'], 'L0_ffn_w2_e': _L0_ffn_in['w2_e'], 'L0_ffn_w1_s': _L0_ffn_in['w1_s'], 'L0_ffn_w3_s': _L0_ffn_in['w3_s'], 'L0_ffn_w2_s': _L0_ffn_in['w2_s']}

def reference(x, cond_512, L0_cond_down_project, L0_cond_down_gamma, L0_cond_down_beta, L0_cond_up_project, L0_cond_up_gamma, L0_cond_up_beta, L0_ffn_gate_W, L0_ffn_w1_e, L0_ffn_w3_e, L0_ffn_w2_e, L0_ffn_w1_s, L0_ffn_w3_s, L0_ffn_w2_s):
    import jax
    import jax.numpy as jnp

    def _L0_cond_ref(hidden_states, conditions, down_project, down_gamma, down_beta, up_project, up_gamma, up_beta):
        import jax, jax.numpy as jnp
        import numpy as np
        B, S, D, H, C = (8, 512, 128, 32, 64)
        INIT_RANGE = 0.01
        dg = conditions @ down_gamma
        db = conditions @ down_beta
        ug = conditions @ up_gamma
        ub = conditions @ up_beta
        w_down = down_project[None, :, :] * dg[:, None, :] + db[:, None, :]
        down = jnp.einsum('bsd,bdh->bsh', hidden_states, w_down)
        act = jax.nn.relu(down)
        w_up = up_project[None, :, :] * ug[:, None, :] + ub[:, None, :]
        up = jnp.einsum('bsh,bhd->bsd', act, w_up)
        return up + hidden_states

    def _L0_ffn_ref(hidden_states, gate_W, w1_e, w3_e, w2_e, w1_s, w3_s, w2_s):
        import jax, jax.numpy as jnp
        import numpy as np
        B, S, D, F, E, NS, K = (2, 128, 128, 512, 8, 8, 2)
        FS = F // NS
        b, s, d = hidden_states.shape
        e = gate_W.shape[0]
        flat = hidden_states.reshape(-1, d)
        T = flat.shape[0]
        logits = (flat @ gate_W.T).astype(jnp.float32)
        probs = jax.nn.softmax(logits, axis=-1)
        top_v, top_i = jax.lax.top_k(probs, K)
        gates = jnp.zeros((T, e), probs.dtype).at[jnp.arange(T)[:, None], top_i].set(top_v)
        g = jax.nn.silu(jnp.einsum('td,edf->etf', flat, w1_e))
        u = jnp.einsum('td,edf->etf', flat, w3_e)
        out_e = jnp.einsum('etf,efd->etd', g * u, w2_e)
        routed = jnp.einsum('te,etd->td', gates, out_e).reshape(b, s, d)
        gs = jax.nn.silu(jnp.einsum('bsd,ndf->nbsf', hidden_states, w1_s))
        us = jnp.einsum('bsd,ndf->nbsf', hidden_states, w3_s)
        shared = jnp.einsum('nbsf,nfd->bsd', gs * us, w2_s) / w1_s.shape[0]
        alpha = 0.5
        return alpha * shared + (1.0 - alpha) * routed
    x = x + _L0_ffn_ref(_L0_cond_ref(x, cond_512, L0_cond_down_project, L0_cond_down_gamma, L0_cond_down_beta, L0_cond_up_project, L0_cond_up_gamma, L0_cond_up_beta), L0_ffn_gate_W, L0_ffn_w1_e, L0_ffn_w3_e, L0_ffn_w2_e, L0_ffn_w1_s, L0_ffn_w3_s, L0_ffn_w2_s)
    return x

_drawn_inputs = setup_inputs


def setup_inputs(seed=0):
    import zlib

    import numpy as np

    out = dict(_drawn_inputs(seed))
    spreads = {'L0_cond_down_beta': (0.0, 0.1), 'L0_cond_up_beta': (0.0, 0.1)}
    factors = {}
    for name, (base, spread) in spreads.items():
        noise = np.random.default_rng([zlib.crc32(name.encode()), seed]).standard_normal(out[name].shape)
        drawn = base * np.exp(spread * noise) if base else spread * noise
        out[name] = jnp.asarray(drawn.astype(out[name].dtype))
    for name, factor in factors.items():
        out[name] = (out[name] * factor).astype(out[name].dtype)
    return out
```

```python
from contextlib import ExitStack

import concourse.bass as bass
from concourse import mybir

F32 = mybir.dt.float32
F32R = mybir.dt.float32r
BF16 = mybir.dt.bfloat16
I32 = mybir.dt.int32
U32 = mybir.dt.uint32
ALU = mybir.AluOpType
ACT = mybir.ActivationFunctionType
AX = mybir.AxisListType.X

P = 128
TOPK = 2


def build(nc, x, x_cols, cond, mods, down_project, up_project, gate, w13, w2, out):
    B, S, D = x.shape
    C = cond.shape[0]
    H = down_project.shape[1]
    E = gate.shape[1]
    F = w13.shape[2] // 2
    T = B * S
    TT = T // P
    TB = S // P
    FC = F // P
    SHARED = E
    RT = TOPK * TT + E - 1
    NT = TT + RT
    RTP = RT + RT % 2
    ALPHA = 0.5
    GATE_SHARED = ALPHA / E
    M = mods.shape[1]
    assert D == P and F == 512 and NT == 31

    with ExitStack() as ctx:
        def sb(name, shape, dt=F32):
            return ctx.enter_context(nc.sbuf_tensor(name, shape, dt))

        def psum(name, shape, dt=F32):
            return ctx.enter_context(nc.psum_tensor(name, shape, dt))

        def sem(name):
            return ctx.enter_context(nc.semaphore(name))

        x2_rows = nc.dram_tensor("x2_rows", [T, D], F32, kind="Internal").ap()
        sum_b = nc.dram_tensor("sum_b", [T + P, D], F32, kind="Internal").ap()
        sums = [out, sum_b]

        raw = sb("raw", [P, 2, 3 * F])
        w13_hi = sb("w13_hi", [P, E + 1, 2 * F], F32R)
        w13_lo = sb("w13_lo", [P, E + 1, 2 * F], F32R)
        w2_parts = sb("w2_parts", [P, E + 1, FC, 2, D], F32R)
        xT = sb("xT", [P, T])
        x_tok = sb("x_tok", [P, TT, D])
        cond_sb = sb("cond_sb", [C, B])
        cond_wide = sb("cond_wide", [C, B, P])
        mods_sb = sb("mods_sb", [C, M])
        dp_sb = sb("dp_sb", [P, H])
        up_sb = sb("up_sb", [H, D])
        gate_sb = sb("gate_sb", [P, E])
        w_down = sb("w_down", [P, B, H])
        w_up = sb("w_up", [H, B, D])
        act_sb = sb("act_sb", [H, T])
        x2T = sb("x2T", [P, T])
        x2_tok = sb("x2_tok", [P, TT, D])
        ident = sb("ident", [P, P])
        zeros = sb("zeros", [P, (T + P) // P * D])
        desc = sb("desc", [P, E])
        thresholds = sb("thresholds", [P, TT])
        tile_iota = sb("tile_iota", [P, RTP])
        slot_iota = sb("slot_iota", [P, P])
        token_iota = sb("token_iota", [P, TT])
        dump_row = sb("dump_row", [P, 1])
        before = sb("before", [P, P], BF16)
        ones = sb("ones", [P, P], BF16)
        shifted = sb("shifted", [P, TT, E])
        exps = sb("exps", [P, TT, E])
        probs = sb("probs", [P, 2, TT, E])
        col = sb("col", [P, 6, TT])
        eq = sb("eq", [P, TT, E])
        cand = sb("cand", [P, TT, E])
        chosen = sb("chosen", [P, TOPK, TT, E])
        sel = sb("sel", [P, TT, E], BF16)
        pre = sb("pre", [P, 4, 4 + TT, E])
        filled = sb("filled", [P, E, TT])
        base = sb("base", [P, 4, 4 + E])
        rank = sb("rank", [P, TT, E])
        pos_all = sb("pos_all", [P, TOPK, TT, E])
        pos_f = sb("pos_f", [P, TOPK * TT])
        pos = sb("pos", [P, TOPK * TT], I32)
        in_tile = sb("in_tile", [P, TOPK * TT], I32)
        tile_at = sb("tile_at", [P, TOPK * TT], I32)
        hot_slot = sb("hot_slot", [P, TOPK * TT, P], F32R)
        hot_tile = sb("hot_tile", [P, TOPK * TT, RTP])
        payload = sb("payload", [P, TOPK * TT, 3], F32R)
        spread = sb("spread", [P, TOPK * TT, 3, RTP], F32R)
        slot_info = sb("slot_info", [P, 3, RTP])
        passed = sb("passed", [P, RTP, E])
        expert_of = sb("expert_of", [P, 2, RTP])
        empty = sb("empty", [P, RTP])
        src_f = sb("src_f", [P, RTP])
        dst_f = sb("dst_f", [P, RTP])
        src_idx = sb("src_idx", [P, TT + RTP], U32)
        dst_idx = sb("dst_idx", [P, TT + RTP], U32)
        slot_gate = sb("slot_gate", [P, TT + RTP])
        tile_expert = sb("tile_expert", [P, TT + RTP], I32)
        xg = sb("xg", [P, 2, D])
        xh = sb("xh", [P, 2, P], F32R)
        xl = sb("xl", [P, 2, P], F32R)
        silu = sb("silu", [P, 2, F])
        h = sb("h", [P, 2, F])
        hh = sb("hh", [P, 2, F], F32R)
        hl = sb("hl", [P, 2, F], F32R)
        y_main = sb("y_main", [P, 2, D])
        y = sb("y", [P, 2, D])

        gu = psum("gu", [P, 4, 512])
        hT = psum("hT", [P, 2, 512])
        px = psum("px", [P, 512])
        py = psum("py", [P, 512])

        loaded_small = sem("loaded_small")
        loaded_x = sem("loaded_x")
        loaded_rows = sem("loaded_rows")
        raw_loaded = [sem(f"raw_loaded{s}") for s in range(2)]
        consts = sem("consts")
        zeroed = sem("zeroed")
        up_scaled = sem("up_scaled")
        sums_set = sem("sums_set")
        front = sem("front")
        front_pe = sem("front_pe")
        front_act = sem("front_act")
        prep_hi = sem("prep_hi")
        prep_lo = sem("prep_lo")
        x2_stored = sem("x2_stored")
        gathered = [sem(f"gathered{s}") for s in range(2)]
        scattered = [sem(f"scattered{s}") for s in range(2)]
        xT_done = sem("xT_done")
        xh_done = sem("xh_done")
        xl_done = sem("xl_done")
        g_done = sem("g_done")
        u_done = sem("u_done")
        silu_done = sem("silu_done")
        h_done = sem("h_done")
        hT_done = sem("hT_done")
        hh_done = sem("hh_done")
        hl_done = sem("hl_done")
        y_done = sem("y_done")
        y_main_done = sem("y_main_done")
        y_out = sem("y_out")
        merged = sem("merged")
        front_all = sem("front_all")

        N_ZERO = 3
        FRONT_W = 4
        block = ctx.enter_context(nc.Block())

        def tile_loop(eng, first, last, step):
            n = (last - first + 1) // 2
            with eng.Fori(0, n) as i:
                for k in range(2):
                    step(2 * i + (first + k), i + (first + k) // 2, (first + k) % 2)
            if (last - first + 1) % 2:
                step(last, last // 2, last % 2)

        @block.sync
        def _(sp):
            sp.dma_start(cond_sb[:], cond).then_inc(loaded_small, 16)
            sp.dma_start(mods_sb[:], mods).then_inc(loaded_small, 16)
            sp.dma_start(dp_sb[:], down_project).then_inc(loaded_small, 16)
            sp.dma_start(up_sb[:], up_project).then_inc(loaded_small, 16)
            sp.dma_start(gate_sb[:], gate).then_inc(loaded_small, 16)
            sp.dma_start(xT[:], x_cols).then_inc(loaded_x, 16)
            sp.dma_start(x_tok[:], x.rearrange("b (j p) d -> p (b j) d", p=P)).then_inc(loaded_rows, 16)
            for n in range(E + 1):
                e = SHARED if n == 0 else n - 1
                if n >= 2:
                    sp.wait_ge(prep_lo, n - 1)
                sp.dma_start(raw[:, n % 2, 0:2 * F], w13[:, e]).then_inc(raw_loaded[n % 2], 16)
                sp.dma_start(raw[:, n % 2, 2 * F:3 * F], w2[:, e]).then_inc(raw_loaded[n % 2], 16)
                if n == 1:
                    sp.wait_ge(zeroed, 1)
                    sp.dma_start(out[0:T], x.rearrange("b s d -> (b s) d")).then_inc(sums_set, 16)
                    sp.dma_start(out[T:T + P], zeros[:, 0:D]).then_inc(sums_set, 16)
                    sp.dma_start(sum_b.rearrange("(p a) d -> p (a d)", p=P), zeros[:]).then_inc(sums_set, 16)
            sp.wait_ge(front, FRONT_W + 4)
            sp.dma_start(x2_rows.rearrange("(j p) d -> p j d", p=P), x2_tok[:]).then_inc(x2_stored, 16)
            sp.wait_ge(sums_set, 16 * 3)
            sp.wait_ge(x2_stored, 16)

        @block.gpsimd
        def _(pool):
            nc.gpsimd.memset(zeros[:], 0.0).then_inc(zeroed, 1)
            nc.gpsimd.memset(ident[:], 0.0).then_inc(consts, 1)
            nc.gpsimd.memset(before[:], 0.0).then_inc(consts, 1)
            nc.gpsimd.memset(ones[:], 1.0).then_inc(consts, 1)
            pool.wait_ge(consts, 3)
            nc.gpsimd.affine_select(out=ident[:], in_=ident[:], compare_op=ALU.not_equal, fill=1.0,
                                    base=0, pattern=[[-1, P]], channel_multiplier=1).then_inc(consts, 1)
            nc.gpsimd.affine_select(out=before[:], in_=before[:], compare_op=ALU.is_ge, fill=1.0,
                                    base=0, pattern=[[-1, P]], channel_multiplier=1).then_inc(consts, 1)
            for ap, pattern, start, per_partition in (
                (desc[:], [[-1, E]], E, 0),
                (thresholds[:], [[P, TT]], 0, 0),
                (tile_iota[:], [[1, RTP]], 0, 0),
                (slot_iota[:], [[1, P]], 0, 0),
                (token_iota[:], [[P, TT]], 1, 1),
                (dump_row[:], [[0, 1]], T + 1, 1),
                (src_idx[:, 0:TT], [[P, TT]], 0, 1),
                (dst_idx[:, 0:TT], [[P, TT]], 0, 1),
                (tile_expert[:, 0:TT], [[0, TT]], SHARED, 0),
            ):
                nc.gpsimd.iota(ap, pattern=pattern, base=start, channel_multiplier=per_partition,
                               allow_small_or_imprecise_dtypes=True).then_inc(consts, 1)
            nc.gpsimd.memset(slot_gate[:, 0:TT], GATE_SHARED).then_inc(consts, 1)

            def gather(t):
                if t >= 2:
                    pool.wait_ge(xT_done, t - 1)
                nc.gpsimd.indirect_dma_start(
                    out=xg[:, t % 2], out_offset=None, in_=x2_rows,
                    in_offset=bass.IndirectOffsetOnAxis(ap=src_idx[:, t:t + 1], axis=0),
                ).then_inc(gathered[t % 2], 16)

            def scatter_add(t):
                pool.wait_ge(y_out, t + 1)
                if t >= 2:
                    pool.wait_ge(scattered[t % 2], 16 * (t // 2))
                nc.gpsimd.indirect_dma_start(
                    out=sums[t % 2], out_offset=bass.IndirectOffsetOnAxis(ap=dst_idx[:, t:t + 1], axis=0),
                    in_=y[:, t % 2], in_offset=None, compute_op=ALU.add,
                ).then_inc(scattered[t % 2], 16)

            pool.wait_ge(consts, 15)
            pool.wait_ge(x2_stored, 16)
            gather(0)
            gather(1)
            pool.wait_ge(sums_set, 16 * 3)
            pool.wait_ge(front_all, 1)
            gather(2)
            for t in range(NT):
                if t + 3 < NT:
                    gather(t + 3)
                scatter_add(t)
            pool.wait_ge(scattered[0], 16 * ((NT + 1) // 2))
            pool.wait_ge(scattered[1], 16 * (NT // 2))
            pool.dma_start(out[0:T], sum_b[0:T], accum_op=ALU.add,
                           max_dma_last_dim=8192).then_inc(merged, 16)
            pool.wait_ge(merged, 16)

        @block.scalar
        def _(act):
            act.wait_ge(front_pe, 2)
            nc.scalar.activation(act_sb[:, 0:S], gu[0:H, 2], ACT.Relu).then_inc(front_act, 1)
            nc.scalar.activation(act_sb[:, S:T], gu[0:H, 3], ACT.Relu).then_inc(front_act, 1)
            act.wait_ge(front, FRONT_W + 6)
            nc.scalar.activation(exps[:], shifted[:], ACT.Exp).then_inc(front_act, 1)
            for n in range(E + 1):
                e = SHARED if n == 0 else n - 1
                act.wait_ge(raw_loaded[n % 2], 32 * (n // 2 + 1))
                nc.scalar.activation(w13_hi[:, e], raw[:, n % 2, 0:2 * F], ACT.Copy)
                nc.scalar.activation(w2_parts[:, e, :, 0], raw[:, n % 2, 2 * F:3 * F].rearrange(
                    "p (c d) -> p c d", c=FC), ACT.Copy).then_inc(prep_hi, 1)

            def split_x(t, s):
                act.wait_ge(xT_done, t + 1)
                nc.scalar.activation(xh[:, s], px[:, 0:P], ACT.Copy).then_inc(xh_done, 1)

            def silu_g(t, s):
                act.wait_ge(g_done, t + 1)
                nc.scalar.activation(silu[:, s], gu[:, s], ACT.Silu).then_inc(silu_done, 1)

            def split_h(t, s):
                act.wait_ge(hT_done, t + 1)
                nc.scalar.activation(hh[:, s], hT[:, s], ACT.Copy).then_inc(hh_done, 1)

            split_x(0, 0)
            silu_g(0, 0)
            split_x(1, 1)

            def step(t, half, s):
                silu_g(t, s)
                split_x(t + 1, 1 - s)
                split_h(t - 1, 1 - s)
            tile_loop(act, 1, NT - 2, step)
            silu_g(NT - 1, (NT - 1) % 2)
            split_h(NT - 2, (NT - 2) % 2)
            split_h(NT - 1, (NT - 1) % 2)

        @block.vector
        def _(dve):
            step_no = [0]

            def chain(ins, wait=True):
                step_no[0] += 1
                ins.then_inc(front, 1)
                if wait:
                    dve.wait_ge(front, step_no[0])

            tt, ts, stt = nc.vector.tensor_tensor, nc.vector.tensor_scalar, nc.vector.scalar_tensor_tensor
            dve.wait_ge(loaded_small, 16 * 5)
            nc.vector.tensor_copy(cond_wide[:], cond_sb[:].unsqueeze(2).to_broadcast([C, B, P])).then_inc(front, 1)
            step_no[0] = 1
            dve.wait_ge(front_pe, 1)
            chain(tt(w_down[:], gu[:, 0:2, 0:H], dp_sb[:].unsqueeze(1).to_broadcast([P, B, H]), ALU.mult))
            chain(tt(w_down[:], w_down[:], gu[:, 0:2, H:2 * H], ALU.add), wait=False)
            nc.vector.tensor_tensor(w_up[:], gu[0:H, 0:2, 2 * H:2 * H + D],
                                    up_sb[:].unsqueeze(1).to_broadcast([H, B, D]), ALU.mult).then_inc(up_scaled, 1)
            dve.wait_ge(up_scaled, 1)
            chain(tt(w_up[:], w_up[:], gu[0:H, 0:2, 2 * H + D:2 * H + 2 * D], ALU.add), wait=False)
            assert step_no[0] == FRONT_W
            dve.wait_ge(loaded_x, 16)
            dve.wait_ge(front_pe, 3)
            chain(tt(x2T[:, 0:S], hT[:, 0], xT[:, 0:S], ALU.add), wait=False)
            dve.wait_ge(front_pe, 4)
            chain(tt(x2T[:, S:T], hT[:, 1], xT[:, S:T], ALU.add), wait=False)
            dve.wait_ge(front_pe, 5)
            dve.wait_ge(loaded_rows, 16)
            for b in range(B):
                chain(tt(x2_tok[:, TB * b:TB * b + TB], gu[:, b].rearrange("p (j d) -> p j d", j=TB),
                         x_tok[:, TB * b:TB * b + TB], ALU.add), wait=False)

            def wide(a):
                return a.unsqueeze(2).to_broadcast([P, TT, E])
            logits = px[:, 0:TT * E].rearrange("p (j e) -> p j e", e=E)
            desc_w = desc[:].unsqueeze(1).to_broadcast([P, TT, E])
            dve.wait_ge(front_pe, 6)
            chain(nc.vector.tensor_reduce(col[:, 0], logits, AX, ALU.max))
            chain(tt(shifted[:], logits, wide(col[:, 0]), ALU.subtract))
            dve.wait_ge(front_act, 3)
            chain(nc.vector.tensor_reduce(col[:, 1], exps[:], AX, ALU.add))
            chain(nc.vector.reciprocal(col[:, 2], col[:, 1]))
            chain(tt(probs[:, 0], exps[:], wide(col[:, 2]), ALU.mult))
            dve.wait_ge(consts, 15)
            for k in range(TOPK):
                chain(nc.vector.tensor_reduce(col[:, 3 + k], probs[:, k], AX, ALU.max))
                chain(tt(eq[:], probs[:, k], wide(col[:, 3 + k]), ALU.is_equal))
                chain(tt(cand[:], eq[:], desc_w, ALU.mult))
                chain(nc.vector.tensor_reduce(col[:, 5], cand[:], AX, ALU.max))
                chain(tt(chosen[:, k], cand[:], wide(col[:, 5]), ALU.is_equal))
                if k == 0:
                    chain(stt(probs[:, 1], chosen[:, 0], -4.0, probs[:, 0], ALU.mult, ALU.add))
            chain(nc.vector.memset(pre[:], 0.0), wait=False)
            chain(nc.vector.memset(base[:], 0.0), wait=False)
            chain(tt(sel[:], chosen[:, 0], chosen[:, 1], ALU.add), wait=False)
            sel_step = step_no[0]
            assert sel_step == SEL_STEP, sel_step
            dve.wait_ge(front_pe, 7)
            counts = py[:, 0:2 * TT * E].rearrange("p (k j e) -> p k j e", k=2, e=E)
            chain(nc.vector.tensor_copy(pre[:, 0, 4:], counts[:, 1]))
            for n, sh in enumerate((1, 2, 4)):
                chain(tt(pre[:, n + 1, 4:], pre[:, n, 4:], pre[:, n, 4 - sh:4 - sh + TT], ALU.add))
            chain(tt(filled[:], pre[:, 3, 4 + TT - 1].unsqueeze(2).to_broadcast([P, E, TT]),
                     thresholds[:].unsqueeze(1).to_broadcast([P, E, TT]), ALU.is_gt))
            chain(nc.vector.tensor_reduce(base[:, 0, 4:], filled[:], AX, ALU.add))
            for n, sh in enumerate((1, 2, 4)):
                chain(tt(base[:, n + 1, 4:], base[:, n, 4:], base[:, n, 4 - sh:4 - sh + E], ALU.add))
            chain(tt(rank[:], counts[:, 0], pre[:, 3, 3:3 + TT], ALU.add))
            chain(stt(rank[:], base[:, 3, 3:3 + E].unsqueeze(1).to_broadcast([P, TT, E]), float(P), rank[:],
                      ALU.mult, ALU.add))
            for k in range(TOPK):
                chain(tt(pos_all[:, k], chosen[:, k], rank[:], ALU.mult))
            chain(nc.vector.tensor_reduce(pos_f[:], pos_all[:].rearrange("p k j e -> p (k j) e"), AX, ALU.add))
            chain(nc.vector.tensor_copy(pos[:], pos_f[:]))
            chain(ts(in_tile[:], pos[:], P - 1, None, ALU.bitwise_and), wait=False)
            chain(ts(tile_at[:], pos[:], P.bit_length() - 1, None, ALU.logical_shift_right))
            NP = TOPK * TT
            chain(tt(hot_tile[:], tile_at[:].unsqueeze(2).to_broadcast([P, NP, RTP]),
                     tile_iota[:].unsqueeze(1).to_broadcast([P, NP, RTP]), ALU.is_equal), wait=False)
            chain(ts(col[:, 3:5], col[:, 3:5], 1.0 - ALPHA, None, ALU.mult))
            for k in range(TOPK):
                chain(nc.vector.tensor_copy(payload[:, TT * k:TT * k + TT, 0], token_iota[:]), wait=False)
            gates2 = col[:, 3:5].rearrange("p k j -> p (k j)")
            chain(nc.vector.tensor_copy(payload[:, :, 1], gates2))
            chain(tt(payload[:, :, 2], gates2, payload[:, :, 1].bitcast(F32), ALU.subtract))
            chain(tt(spread[:], hot_tile[:].unsqueeze(2).to_broadcast([P, NP, 3, RTP]),
                     payload[:].bitcast(F32).unsqueeze(3).to_broadcast([P, NP, 3, RTP]), ALU.mult), wait=False)
            chain(tt(hot_slot[:], in_tile[:].unsqueeze(2).to_broadcast([P, NP, P]),
                     slot_iota[:].unsqueeze(1).to_broadcast([P, NP, P]), ALU.is_equal), wait=False)
            assert step_no[0] == HOT_STEP, step_no[0]
            chain(tt(passed[:], tile_iota[:].unsqueeze(2).to_broadcast([P, RTP, E]),
                     base[:, 3, 4:].unsqueeze(1).to_broadcast([P, RTP, E]), ALU.is_ge))
            chain(nc.vector.tensor_reduce(expert_of[:, 0], passed[:], AX, ALU.add))
            chain(ts(tile_expert[:, TT:], expert_of[:, 0], float(E - 1), None, ALU.min), wait=False)
            dve.wait_ge(front_pe, 8)
            chain(nc.vector.tensor_copy(slot_info[:], px[:, 0:3 * RTP].rearrange("p (c t) -> p c t", c=3)))
            chain(tt(slot_gate[:, TT:], slot_info[:, 1], slot_info[:, 2], ALU.add), wait=False)
            chain(ts(src_idx[:, TT:], slot_info[:, 0], -1.0, 0.0, ALU.add, ALU.max), wait=False)
            chain(ts(empty[:], slot_info[:, 0], 0.0, dump_row[:, 0:1], ALU.is_equal, ALU.mult))
            chain(stt(dst_idx[:, TT:], slot_info[:, 0], -1.0, empty[:], ALU.add, ALU.add), wait=False)
            nc.vector.memset(col[:, 0], 0.0).then_inc(front_all, 1)

            for n in range(E + 1):
                e = SHARED if n == 0 else n - 1
                dve.wait_ge(prep_hi, n + 1)
                tt(w13_lo[:, e], raw[:, n % 2, 0:2 * F], w13_hi[:, e].bitcast(F32), ALU.subtract)
                tt(w2_parts[:, e, :, 1], raw[:, n % 2, 2 * F:3 * F].rearrange("p (c d) -> p c d", c=FC),
                   w2_parts[:, e, :, 0].bitcast(F32), ALU.subtract).then_inc(prep_lo, 1)

            def split_x(t, s):
                dve.wait_ge(xh_done, t + 1)
                tt(xl[:, s], px[:, 0:P], xh[:, s].bitcast(F32), ALU.subtract).then_inc(xl_done, 1)

            def mix(t, s):
                dve.wait_ge(u_done, t + 1)
                dve.wait_ge(silu_done, t + 1)
                stt(h[:, s], silu[:, s], slot_gate[:, bass.ds(t, 1)], gu[:, 2 + s], ALU.mult,
                    ALU.mult).then_inc(h_done, 1)

            def split_h(t, s):
                dve.wait_ge(hh_done, t + 1)
                tt(hl[:, s], hT[:, s], hh[:, s].bitcast(F32), ALU.subtract).then_inc(hl_done, 1)

            def y_rows(t, half, s, first=False):
                dve.wait_ge(y_done, t + 1)
                if not first:
                    dve.wait_ge(scattered[s], 16 * half)
                nc.vector.tensor_copy(y_main[:, s], py[:, 0:D]).then_inc(y_main_done, 1)
                dve.wait_ge(y_main_done, t + 1)
                tt(y[:, s], y_main[:, s], py[:, D:2 * D], ALU.add).then_inc(y_out, 1)

            split_x(0, 0)
            mix(0, 0)
            split_x(1, 1)
            mix(1, 1)
            split_x(2, 0)
            split_h(0, 0)
            for t in (2, 3):
                mix(t, t % 2)
                split_x(t + 1, (t + 1) % 2)
                split_h(t - 1, (t - 1) % 2)
                y_rows(t - 2, 0, t % 2, first=True)

            def step(t, half, s):
                mix(t, s)
                split_x(t + 1, 1 - s)
                split_h(t - 1, 1 - s)
                y_rows(t - 2, half - 1, s)
            tile_loop(dve, 4, NT - 2, step)
            mix(NT - 1, (NT - 1) % 2)
            split_h(NT - 2, (NT - 2) % 2)
            y_rows(NT - 3, (NT - 3) // 2, (NT - 3) % 2)
            split_h(NT - 1, (NT - 1) % 2)
            y_rows(NT - 2, (NT - 2) // 2, (NT - 2) % 2)
            y_rows(NT - 1, (NT - 1) // 2, (NT - 1) % 2)

        @block.tensor
        def _(pe):
            mm = nc.tensor.matmul
            pe.wait_ge(front, 1)
            for b in range(B):
                i = mm(gu[:, b, 0:M], cond_wide[:, b], mods_sb[:], start=True, stop=True)
            i.then_inc(front_pe, 1)
            pe.wait_ge(loaded_x, 16)
            pe.wait_ge(front, 3)
            for b in range(B):
                i = mm(gu[0:H, 2 + b], w_down[:, b], xT[:, S * b:S * b + S], start=True, stop=True)
            i.then_inc(front_pe, 1)
            pe.wait_ge(front, FRONT_W)
            for b in range(B):
                pe.wait_ge(front_act, b + 1)
                mm(hT[:, b], w_up[:, b], act_sb[:, S * b:S * b + S], start=True, stop=True).then_inc(front_pe, 1)
            for j in range(TT):
                i = mm(gu[:, j // TB, D * (j % TB):D * (j % TB) + D], act_sb[:, P * j:P * j + P], w_up[:, j // TB],
                       start=True, stop=True)
            i.then_inc(front_pe, 1)
            pe.wait_ge(front, FRONT_W + 2)
            for j in range(TT):
                i = mm(px[:, E * j:E * j + E], x2T[:, P * j:P * j + P], gate_sb[:], start=True, stop=True)
            i.then_inc(front_pe, 1)
            pe.wait_ge(front, SEL_STEP)
            sel2 = sel[:].rearrange("p j e -> p (j e)")
            mm(py[:, 0:TT * E], before[:], sel2, start=True, stop=True)
            mm(py[:, TT * E:2 * TT * E], ones[:], sel2, start=True, stop=True).then_inc(front_pe, 1)
            pe.wait_ge(front, HOT_STEP)
            for n in range(TOPK * TT):
                i = mm(px[:, 0:3 * RTP], hot_slot[:, n], spread[:, n].rearrange("p c t -> p (c t)"),
                       start=(n == 0), stop=(n == TOPK * TT - 1))
            i.then_inc(front_pe, 1)

            def transpose_x(t, s, count):
                pe.wait_ge(gathered[s], count)
                nc.tensor.transpose(px[:, 0:P], xg[:, s], ident[:]).then_inc(xT_done, 1)

            def layer1(t, s):
                e = pe.value_load(tile_expert[0:1, bass.ds(t, 1)], min_val=0, max_val=E)
                pe.wait_ge(xl_done, t + 1)
                for part, done in ((0, g_done), (1, u_done)):
                    acc = gu[:, 2 * part + s]
                    cols = slice(part * F, part * F + F)
                    mm(acc, xh[:, s], w13_hi[:, bass.ds(e, 1), cols], start=True, stop=False)
                    mm(acc, xh[:, s], w13_lo[:, bass.ds(e, 1), cols], start=False, stop=False)
                    mm(acc, xl[:, s], w13_hi[:, bass.ds(e, 1), cols], start=False, stop=True).then_inc(done, 1)

            def transpose_h(t, s):
                pe.wait_ge(h_done, t + 1)
                for c in range(FC):
                    i = nc.tensor.transpose(hT[:, s, P * c:P * c + P], h[:, s, P * c:P * c + P], ident[:])
                i.then_inc(hT_done, 1)

            def layer2(t, s, first=False):
                e = pe.value_load(tile_expert[0:1, bass.ds(t, 1)], min_val=0, max_val=E)
                pe.wait_ge(hl_done, t + 1)
                if not first:
                    pe.wait_ge(y_out, t)
                for c in range(FC):
                    f = slice(P * c, P * c + P)
                    mm(py[:, 0:2 * D], hh[:, s, f],
                       w2_parts[:, bass.ds(e, 1), c].rearrange("p e k d -> p (e k d)"), start=(c == 0), stop=False)
                    i = mm(py[:, 0:D], hl[:, s, f],
                           w2_parts[:, bass.ds(e, 1), c, 0].rearrange("p e d -> p (e d)"), start=False, stop=(c == FC - 1))
                i.then_inc(y_done, 1)

            pe.wait_ge(front_all, 1)
            pe.wait_ge(prep_lo, E + 1)
            transpose_x(0, 0, 16)
            layer1(0, 0)
            transpose_x(1, 1, 16)
            layer1(1, 1)
            transpose_x(2, 0, 32)
            transpose_h(0, 0)
            layer1(2, 0)
            transpose_x(3, 1, 32)
            transpose_h(1, 1)
            layer2(0, 0, first=True)

            def step(t, half, s):
                layer1(t, s)
                transpose_x(t + 1, 1 - s, 16 * ((half + 1) if s == 0 else (half + 2)))
                transpose_h(t - 1, 1 - s)
                layer2(t - 2, s)
            tile_loop(pe, 3, NT - 2, step)
            layer1(NT - 1, (NT - 1) % 2)
            transpose_h(NT - 2, (NT - 2) % 2)
            layer2(NT - 3, (NT - 3) % 2)
            transpose_h(NT - 1, (NT - 1) % 2)
            layer2(NT - 2, (NT - 2) % 2)
            layer2(NT - 1, (NT - 1) % 2)


SEL_STEP = 27
HOT_STEP = 52


def kernel(**inputs):
    import numpy as np
    import concourse.bacc as bacc
    from concourse.bass_utils import run_bass_kernel_spmd

    given = {k: np.asarray(v) for k, v in inputs.items()}
    x = given["x"]
    B, S, D = x.shape
    E, _, F = given["L0_ffn_w1_e"].shape
    w1_s, w3_s, w2_s = (given["L0_ffn_" + n] for n in ("w1_s", "w3_s", "w2_s"))
    w1 = np.concatenate([given["L0_ffn_w1_e"].transpose(1, 0, 2), w1_s.transpose(1, 0, 2).reshape(D, 1, F)], axis=1)
    w3 = np.concatenate([given["L0_ffn_w3_e"].transpose(1, 0, 2), w3_s.transpose(1, 0, 2).reshape(D, 1, F)], axis=1)
    w2 = np.concatenate([given["L0_ffn_w2_e"], w2_s.reshape(1, F, D)], axis=0)
    laid = {
        "x": x,
        "x_cols": x.reshape(B * S, D).T,
        "cond": given["cond_512"].T,
        "mods": np.concatenate([given["L0_cond_" + n] for n in ("down_gamma", "down_beta", "up_gamma", "up_beta")], axis=1),
        "down_project": given["L0_cond_down_project"],
        "up_project": given["L0_cond_up_project"],
        "gate": given["L0_ffn_gate_W"].T,
        "w13": np.concatenate([w1, w3], axis=2),
        "w2": w2.reshape(E + 1, F // 128, 128, D).transpose(2, 0, 1, 3).reshape(128, E + 1, F // 128 * D),
    }
    nc = bacc.Bacc("TRN2", target_bir_lowering=False, num_devices=1)
    arrays, args = {}, []
    for name, a in laid.items():
        a = np.ascontiguousarray(a)
        arrays["in_" + name] = a
        args.append(nc.dram_tensor("in_" + name, a.shape, mybir.dt.from_np(a.dtype), kind="ExternalInput").ap())
    args.append(nc.dram_tensor("out_0", (B * S + 128, D), F32, kind="ExternalOutput").ap())
    build(nc, *args)
    result = run_bass_kernel_spmd(nc, [arrays], core_ids=[0]).results[0]["out_0"]
    return result[:B * S].reshape(B, S, D)
```

```python
from contextlib import ExitStack

import concourse.bass as bass
from concourse import mybir

F32 = mybir.dt.float32
F32R = mybir.dt.float32r
BF16 = mybir.dt.bfloat16
I32 = mybir.dt.int32
U32 = mybir.dt.uint32
ALU = mybir.AluOpType
ACT = mybir.ActivationFunctionType
AX = mybir.AxisListType.X

P = 128
TOPK = 2
RING = 4
RAW = 3
LO_ON_VECTOR = (0, 3, 6)


def build(nc, x, x_cols, params, w13, w2, out):
    B, S, D = x.shape
    T = B * S
    TT = T // P
    TB = S // P
    E = w13.shape[1] - 1
    F = w13.shape[2] // 2
    FC = F // P
    H = 32
    C = 64
    SHARED = E
    UNITS = B * FC
    NT = TOPK * TT + E - 1
    NTP = NT + NT % 2
    PAIRS = TOPK * TT
    ALPHA = 0.5
    GATE_SHARED = ALPHA / E
    MODS = 2 * H + 2 * D
    AT_MODS, AT_COND, AT_DOWN, AT_UP = 0, MODS, MODS + B, MODS + B + H
    AT_GATE = AT_UP + D
    assert D == P and S == F == 512 and UNITS == 8 and NT == 23 and AT_GATE + E == params.shape[1]

    with ExitStack() as ctx:
        def sb(name, shape, dt=F32):
            return ctx.enter_context(nc.sbuf_tensor(name, shape, dt))

        def psum(name, shape, dt=F32):
            return ctx.enter_context(nc.psum_tensor(name, shape, dt))

        def sem(name):
            return ctx.enter_context(nc.semaphore(name))

        x2_rows = nc.dram_tensor("x2_rows", [T, 2 * D], F32R, kind="Internal").ap()
        sum_b = nc.dram_tensor("sum_b", [T + P, D], F32, kind="Internal").ap()
        sums = [out, sum_b]

        raw = sb("raw", [P, RAW, 3 * F])
        w13_hi = sb("w13_hi", [P, E + 1, 2 * F], F32R)
        w13_lo = sb("w13_lo", [P, E + 1, 2 * F], F32R)
        w2_parts = sb("w2_parts", [P, E + 1, FC, 2, D], F32R)
        pr = sb("pr", [P, params.shape[1]])
        xT = sb("xT", [P, T])
        x_tok = sb("x_tok", [P, TT, D])
        cond_wide = sb("cond_wide", [C, B, P])
        w_down = sb("w_down", [P, B, H])
        w_up = sb("w_up", [H, B, D])
        small = sb("small", [P, T])
        inner = small[0:H]
        yT = small[:, 0:S]
        x2T = sb("x2T", [P, T])
        x2h = sb("x2h", [P, T], F32R)
        x2l = sb("x2l", [P, T], F32R)
        x2_parts = sb("x2_parts", [P, TT, 2, D], F32R)
        ident = sb("ident", [P, P])
        ident_r = sb("ident_r", [P, P], F32R)
        zeros = sb("zeros", [P, D])
        warm = sb("warm", [P, 512], BF16)
        desc = sb("desc", [P, E])
        thresholds = sb("thresholds", [P, TT])
        tile_iota = sb("tile_iota", [P, NTP])
        slot_iota = sb("slot_iota", [P, P])
        token_iota = sb("token_iota", [P, TT])
        dump_row = sb("dump_row", [P, 1])
        before = sb("before", [P, P], BF16)
        ones = sb("ones", [P, P], BF16)
        top = sb("top", [P, TOPK, TT])
        below = sb("below", [P, TOPK, TT, E])
        left = sb("left", [P, TT, E])
        cand = sb("cand", [P, TT, E])
        best = sb("best", [P, TT])
        chosen = sb("chosen", [P, TOPK, TT, E])
        sel = sb("sel", [P, TT, E], BF16)
        exps = sb("exps", [P, TT, E])
        exp_second = sb("exp_second", [P, TT])
        total = sb("total", [P, TT])
        gates = sb("gates", [P, TOPK, TT])
        filled = sb("filled", [P, E, TT])
        base = sb("base", [P, 4, 4 + E])
        place = sb("place", [P, TT, E])
        place_of = sb("place_of", [P, TOPK, TT, E])
        pos_f = sb("pos_f", [P, PAIRS])
        pos = sb("pos", [P, PAIRS], I32)
        in_tile = sb("in_tile", [P, PAIRS], I32)
        tile_at = sb("tile_at", [P, PAIRS], I32)
        hot_slot = sb("hot_slot", [P, PAIRS, P], F32R)
        hot_tile = sb("hot_tile", [P, PAIRS, NTP])
        payload = sb("payload", [P, PAIRS, 3], F32R)
        spread = sb("spread", [P, PAIRS, 3, NTP], F32R)
        slot_info = sb("slot_info", [P, 3, NTP])
        passed = sb("passed", [P, NTP, E])
        expert_of = sb("expert_of", [P, NTP])
        empty = sb("empty", [P, NTP])
        src_idx = sb("src_idx", [P, NTP], U32)
        dst_idx = sb("dst_idx", [P, NTP], U32)
        slot_gate = sb("slot_gate", [P, NTP])
        tile_expert = sb("tile_expert", [P, NTP], I32)
        xg = sb("xg", [P, RING, 2 * D], F32R)
        xs = sb("xs", [P, 2, 2, P], F32R)
        silu = sb("silu", [P, 2, F])
        h = sb("h", [P, 2, F])
        hh = sb("hh", [P, 2, F], F32R)
        hl = sb("hl", [P, 2, F], F32R)
        y_main = small[:, S:S + 2 * D].rearrange("p (s d) -> p s d", s=2)
        y = small[:, S + 2 * D:S + 4 * D].rearrange("p (s d) -> p s d", s=2)
        shared_rows = xT[:].rearrange("p (j d) -> p j d", d=D)

        gu = psum("gu", [P, 4, 512])
        hT = psum("hT", [P, 2, 512])
        px = psum("px", [P, 512])
        py = psum("py", [P, 512])

        params_in, x_in, rows_in = sem("params_in"), sem("x_in"), sem("rows_in")
        raw_in = [sem(f"raw_in{r}") for r in range(RAW)]
        raw_free = [sem(f"raw_free{r}") for r in range(RAW)]
        consts, consts_step, warm_ready = sem("consts"), sem("consts_step"), sem("warm_ready")
        hi_done = sem("hi_done")
        lo_vector, lo_pool = sem("lo_vector"), sem("lo_pool")
        cond_ready, mods_done, scaled = sem("cond_ready"), sem("mods_done"), sem("scaled")
        down_ready, up_ready = sem("down_ready"), sem("up_ready")
        inner_done, relu_done, adapted = sem("inner_done"), sem("relu_done"), sem("adapted")
        x2_done, x2h_done, x2l_done = sem("x2_done"), sem("x2h_done"), sem("x2l_done")
        rows_turned, rows_done, x2_stored = sem("rows_turned"), sem("rows_done"), sem("x2_stored")
        step_done = sem("step_done")
        logits_done, below_done, second_done, exps_done = (
            sem("logits_done"), sem("below_done"), sem("second_done"), sem("exps_done"))
        sel_done, places_done, hot_done, dispatched = (
            sem("sel_done"), sem("places_done"), sem("hot_done"), sem("dispatched"))
        src_ready, dst_ready, experts_ready = sem("src_ready"), sem("dst_ready"), sem("experts_ready")
        g_done, u_done, silu_done, h_done = sem("g_done"), sem("u_done"), sem("silu_done"), sem("h_done")
        hh_done, hl_done = sem("hh_done"), sem("hl_done")
        yT_done, yT_copied, y_turned, shared_done = (
            sem("yT_done"), sem("yT_copied"), sem("y_turned"), sem("shared_done"))
        gathered = [sem(f"gathered{r}") for r in range(RING)]
        scattered = [sem(f"scattered{s}") for s in range(2)]
        xT_done, xs_done, hT_done, y_done, y_main_done, y_out = (
            sem("xT_done"), sem("xs_done"), sem("hT_done"), sem("y_done"), sem("y_main_done"), sem("y_out"))
        sums_set, zeros_set, merged = sem("sums_set"), sem("zeros_set"), sem("merged")

        block = ctx.enter_context(nc.Block())

        def expert_at(n):
            return SHARED if n == 0 else n - 1

        def tile_loop(eng, first, last, step):
            rounds = (last - first + 1) // RING
            with eng.Fori(0, rounds) as i:
                for k in range(RING):
                    step(RING * i + (first + k), i + (first + k) // RING, (first + k) % RING)
            for t in range(first + RING * rounds, last + 1):
                step(t, t // RING, t % RING)

        @block.sync
        def _(sp):
            sp.dma_start(pr[:], params).then_inc(params_in, 16)
            sp.dma_start(xT[:], x_cols).then_inc(x_in, 16)
            for n in range(E + 1):
                if n >= RAW:
                    sp.wait_ge(raw_free[n % RAW], n // RAW)
                sp.dma_start(raw[:, n % RAW, 0:2 * F], w13[:, expert_at(n)]).then_inc(raw_in[n % RAW], 16)
                sp.dma_start(raw[:, n % RAW, 2 * F:3 * F], w2[:, expert_at(n)]).then_inc(raw_in[n % RAW], 16)
                if n == 2:
                    sp.dma_start(x_tok[:], x.rearrange("b (j p) d -> p (b j) d", p=P)).then_inc(rows_in, 16)
                    sp.wait_ge(consts, 1)
                    sp.dma_start(out[T:T + P], zeros[:]).then_inc(zeros_set, 16)
                    sp.dma_start(sum_b.rearrange("(a p) d -> p a d", p=P),
                                 zeros[:].unsqueeze(1).to_broadcast([P, TT + 1, D])).then_inc(zeros_set, 16)
                if n in (STORE_AFTER, STORE_AFTER + 1):
                    b = n - STORE_AFTER
                    sp.wait_ge(rows_done, b + 1)
                    sp.dma_start(x2_rows.rearrange("(j p) d -> p j d", p=P)[:, TB * b:TB * b + TB].bitcast(F32),
                                 x2_parts[:, TB * b:TB * b + TB].rearrange("p j k d -> p j (k d)").bitcast(F32)
                                 ).then_inc(x2_stored, 16)
            for b in range(B):
                sp.wait_ge(shared_done, b + 1)
                sp.dma_start(out[S * b:S * b + S].rearrange("(j p) d -> p j d", p=P),
                             shared_rows[:, TB * b:TB * b + TB]).then_inc(sums_set, 16)
            sp.wait_ge(sums_set, 16 * B)
            sp.wait_ge(zeros_set, 16 * 2)
            sp.wait_ge(x2_stored, 16 * B)

        @block.gpsimd
        def _(pool):
            nc.gpsimd.memset(warm[:], 0.0).then_inc(warm_ready, 1)
            nc.gpsimd.memset(ident[:], 0.0).then_inc(consts_step, 1)
            nc.gpsimd.memset(before[:], 0.0).then_inc(consts_step, 1)
            nc.gpsimd.memset(ones[:], 1.0).then_inc(consts_step, 1)
            pool.wait_ge(consts_step, 3)
            nc.gpsimd.affine_select(out=ident[:], in_=ident[:], compare_op=ALU.not_equal, fill=1.0,
                                    base=0, pattern=[[-1, P]], channel_multiplier=1).then_inc(consts_step, 1)
            nc.gpsimd.affine_select(out=before[:], in_=before[:], compare_op=ALU.is_ge, fill=1.0,
                                    base=0, pattern=[[-1, P]], channel_multiplier=1).then_inc(consts_step, 1)
            pool.wait_ge(consts_step, 5)
            nc.gpsimd.tensor_copy(ident_r[:], ident[:]).then_inc(consts_step, 1)
            for ap, pattern, start, per_partition in (
                (desc[:], [[-1, E]], E, 0),
                (thresholds[:], [[P, TT]], 0, 0),
                (tile_iota[:], [[1, NTP]], 0, 0),
                (slot_iota[:], [[1, P]], 0, 0),
                (token_iota[:], [[P, TT]], 1, 1),
                (dump_row[:], [[0, 1]], T + 1, 1),
            ):
                nc.gpsimd.iota(ap, pattern=pattern, base=start, channel_multiplier=per_partition,
                               allow_small_or_imprecise_dtypes=True).then_inc(consts_step, 1)
            pool.wait_ge(consts_step, 12)
            nc.gpsimd.memset(zeros[:], 0.0).then_inc(consts, 1)

            for n in range(E + 1):
                if n not in LO_ON_VECTOR:
                    e, r = expert_at(n), n % RAW
                    pool.wait_ge(hi_done, n + 1)
                    nc.gpsimd.tensor_tensor(w13_lo[:, e], raw[:, r, 0:2 * F], w13_hi[:, e].bitcast(F32),
                                            ALU.subtract).then_inc(lo_pool, 1)
                    nc.gpsimd.tensor_tensor(
                        w2_parts[:, e, :, 1], raw[:, r, 2 * F:3 * F].rearrange("p (c d) -> p c d", c=FC),
                        w2_parts[:, e, :, 0].bitcast(F32), ALU.subtract).then_inc(lo_pool, 1)
                    pool.wait_ge(lo_pool, 2 * sum(m not in LO_ON_VECTOR for m in range(n + 1)))
                    nc.gpsimd.sem_inc(raw_free[r], 1)

            def gather(t):
                if t >= RING:
                    pool.wait_ge(xT_done, t - RING + 1)
                nc.gpsimd.indirect_dma_start(
                    out=xg[:, t % RING], out_offset=None, in_=x2_rows,
                    in_offset=bass.IndirectOffsetOnAxis(ap=src_idx[:, t:t + 1], axis=0),
                ).then_inc(gathered[t % RING], 16)

            def scatter_add(t):
                pool.wait_ge(y_out, t + 1)
                if t >= 2:
                    pool.wait_ge(scattered[t % 2], 16 * (t // 2))
                nc.gpsimd.indirect_dma_start(
                    out=sums[t % 2], out_offset=bass.IndirectOffsetOnAxis(ap=dst_idx[:, t:t + 1], axis=0),
                    in_=y[:, t % 2], in_offset=None, compute_op=ALU.add,
                ).then_inc(scattered[t % 2], 16)

            pool.wait_ge(x2_stored, 16 * B)
            pool.wait_ge(src_ready, 1)
            for t in range(RING):
                gather(t)
            pool.wait_ge(dst_ready, 1)
            pool.wait_ge(zeros_set, 16 * 2)
            pool.wait_ge(sums_set, 16 * B)
            for t in range(NT):
                if t + RING < NT:
                    gather(t + RING)
                scatter_add(t)
            pool.wait_ge(scattered[0], 16 * ((NT + 1) // 2))
            pool.wait_ge(scattered[1], 16 * (NT // 2))
            pool.dma_start(out[0:T], sum_b[0:T], accum_op=ALU.add,
                           max_dma_last_dim=8192).then_inc(merged, 16)
            pool.wait_ge(merged, 16)

        @block.scalar
        def _(act):
            def weights_hi(n):
                e, r = expert_at(n), n % RAW
                act.wait_ge(raw_in[r], 32 * (n // RAW + 1))
                nc.scalar.activation(w13_hi[:, e], raw[:, r, 0:2 * F], ACT.Copy)
                nc.scalar.activation(w2_parts[:, e, :, 0], raw[:, r, 2 * F:3 * F].rearrange(
                    "p (c d) -> p c d", c=FC), ACT.Copy).then_inc(hi_done, 1)

            def silu_g(n, s):
                act.wait_ge(g_done, n + 1)
                nc.scalar.activation(silu[:, s], gu[:, s], ACT.Silu).then_inc(silu_done, 1)

            def rows_out(b):
                act.wait_ge(rows_turned, b + 1)
                nc.scalar.activation(x2_parts[:, TB * b:TB * b + TB].rearrange("p j k d -> p (j k d)"),
                                     hT[:].rearrange("p k c -> p (k c)"), ACT.Copy).then_inc(rows_done, 1)

            def unit_hi(u):
                act.wait_ge(h_done, u + 1)
                nc.scalar.activation(hh[:, u % 2], h[:, u % 2], ACT.Copy).then_inc(hh_done, 1)

            def yT_out(b):
                act.wait_ge(yT_done, b + 1)
                if b:
                    act.wait_ge(y_turned, b)
                nc.scalar.activation(yT, hT[:, 0], ACT.Copy).then_inc(yT_copied, 1)

            weights_hi(0)
            for b in range(B):
                act.wait_ge(inner_done, b + 1)
                nc.scalar.activation(inner[:, S * b:S * b + S], gu[0:H, 2 + b], ACT.Relu).then_inc(relu_done, 1)
            for b in range(B):
                act.wait_ge(x2_done, b + 1)
                nc.scalar.activation(x2h[:, S * b:S * b + S], x2T[:, S * b:S * b + S], ACT.Copy).then_inc(x2h_done, 1)
            act.wait_ge(below_done, 1)
            nc.scalar.activation(exps[:], below[:, 0], ACT.Exp).then_inc(exps_done, 1)
            weights_hi(1)
            rows_out(0)
            act.wait_ge(second_done, 1)
            nc.scalar.activation(exp_second[:], top[:, 1], ACT.Exp).then_inc(exps_done, 1)
            silu_g(0, 0)
            rows_out(1)
            weights_hi(2)
            for u in range(1, UNITS):
                unit_hi(u - 1)
                silu_g(u, u % 2)
                if u == FC + 1:
                    yT_out(0)
                if u + 2 <= E:
                    weights_hi(u + 2)

            def split_x(t, s):
                act.wait_ge(xT_done, t + 1)
                nc.scalar.activation(xs[:, s].rearrange("p k q -> p (k q)"), px[:, 0:2 * P],
                                     ACT.Copy).then_inc(xs_done, 1)

            def split_h(t, s):
                act.wait_ge(hT_done, t + 1)
                nc.scalar.activation(hh[:, s], hT[:, s], ACT.Copy).then_inc(hh_done, 1)

            def y_first(t, s):
                act.wait_ge(y_done, t + 1)
                nc.scalar.activation(y_main[:, s], py[:, 0:D], ACT.Copy).then_inc(y_main_done, 1)

            split_x(0, 0)
            unit_hi(UNITS - 1)
            silu_g(UNITS, 0)
            split_x(1, 1)
            yT_out(1)

            def step(t, turn, r):
                s = r % 2
                silu_g(UNITS + t, s)
                split_x(t + 1, 1 - s)
                split_h(t - 1, 1 - s)
                if not isinstance(t, int) or t >= 2:
                    y_first(t - 2, s)
            step(1, 0, 1)
            step(2, 0, 2)
            tile_loop(act, 3, NT - 2, step)
            silu_g(UNITS + NT - 1, (NT - 1) % 2)
            split_h(NT - 2, (NT - 2) % 2)
            y_first(NT - 3, (NT - 3) % 2)
            split_h(NT - 1, (NT - 1) % 2)
            y_first(NT - 2, (NT - 2) % 2)
            y_first(NT - 1, (NT - 1) % 2)

        @block.vector
        def _(dve):
            tt, ts, stt = nc.vector.tensor_tensor, nc.vector.tensor_scalar, nc.vector.scalar_tensor_tensor
            reduce = nc.vector.tensor_reduce
            steps = [0]

            def step_on(ins, wait=True):
                steps[0] += 1
                ins.then_inc(step_done, 1)
                if wait:
                    dve.wait_ge(step_done, steps[0])

            def wide(a):
                return a.unsqueeze(2).to_broadcast([P, TT, E])

            def weights_lo(n):
                e, r = expert_at(n), n % RAW
                dve.wait_ge(hi_done, n + 1)
                tt(w13_lo[:, e], raw[:, r, 0:2 * F], w13_hi[:, e].bitcast(F32), ALU.subtract).then_inc(lo_vector, 1)
                tt(w2_parts[:, e, :, 1], raw[:, r, 2 * F:3 * F].rearrange("p (c d) -> p c d", c=FC),
                   w2_parts[:, e, :, 0].bitcast(F32), ALU.subtract).then_inc(raw_free[r], 1)

            def unit_mix(u):
                dve.wait_ge(u_done, u + 1)
                dve.wait_ge(silu_done, u + 1)
                stt(h[:, u % 2], silu[:, u % 2], GATE_SHARED, gu[:, 2 + u % 2], ALU.mult, ALU.mult).then_inc(h_done, 1)

            def unit_lo(u):
                dve.wait_ge(hh_done, u + 1)
                tt(hl[:, u % 2], h[:, u % 2], hh[:, u % 2].bitcast(F32), ALU.subtract).then_inc(hl_done, 1)

            def shared_out(b):
                dve.wait_ge(y_turned, b + 1)
                tt(shared_rows[:, TB * b:TB * b + TB], py[:].rearrange("p (j d) -> p j d", j=TB),
                   x_tok[:, TB * b:TB * b + TB], ALU.add).then_inc(shared_done, 1)

            dve.wait_ge(params_in, 16)
            nc.vector.tensor_copy(cond_wide[:], pr[0:C, AT_COND:AT_COND + B].unsqueeze(2).to_broadcast([C, B, P])
                                  ).then_inc(cond_ready, 1)
            dve.wait_ge(mods_done, 1)
            tt(w_down[:], gu[:, 0:2, 0:H], pr[:, AT_DOWN:AT_DOWN + H].unsqueeze(1).to_broadcast([P, B, H]),
               ALU.mult).then_inc(scaled, 1)
            tt(w_up[:], gu[0:H, 0:2, 2 * H:2 * H + D], pr[0:H, AT_UP:AT_UP + D].unsqueeze(1).to_broadcast([H, B, D]),
               ALU.mult).then_inc(scaled, 1)
            dve.wait_ge(scaled, 1)
            tt(w_down[:], w_down[:], gu[:, 0:2, H:2 * H], ALU.add).then_inc(down_ready, 1)
            dve.wait_ge(scaled, 2)
            tt(w_up[:], w_up[:], gu[0:H, 0:2, 2 * H + D:2 * H + 2 * D], ALU.add).then_inc(up_ready, 1)
            step_on(nc.vector.memset(base[:], 0.0), wait=False)
            weights_lo(0)
            dve.wait_ge(x_in, 16)
            for b in range(B):
                dve.wait_ge(adapted, b + 1)
                tt(x2T[:, S * b:S * b + S], hT[:, b], xT[:, S * b:S * b + S], ALU.add).then_inc(x2_done, 1)
            for b in range(B):
                dve.wait_ge(x2h_done, b + 1)
                tt(x2l[:, S * b:S * b + S], x2T[:, S * b:S * b + S], x2h[:, S * b:S * b + S].bitcast(F32),
                   ALU.subtract).then_inc(x2l_done, 1)

            dve.wait_ge(consts, 1)
            desc_w = desc[:].unsqueeze(1).to_broadcast([P, TT, E])

            def pick(k, logits, signal):
                step_on(reduce(top[:, k], logits, AX, ALU.max))
                tt(below[:, k], logits, wide(top[:, k]), ALU.subtract).then_inc(signal, 1)
                dve.wait_ge(signal, 1)
                step_on(stt(cand[:], below[:, k], 0.0, desc_w, ALU.is_equal, ALU.mult))
                step_on(reduce(best[:], cand[:], AX, ALU.max))
                step_on(tt(chosen[:, k], cand[:], wide(best[:]), ALU.is_equal))

            dve.wait_ge(logits_done, 1)
            pick(0, px[:, 0:TT * E].rearrange("p (j e) -> p j e", e=E), below_done)
            step_on(stt(left[:], chosen[:, 0], -1e30, below[:, 0], ALU.mult, ALU.add))
            pick(1, left[:], second_done)
            tt(sel[:], chosen[:, 0], chosen[:, 1], ALU.add).then_inc(sel_done, 1)
            unit_mix(0)
            dve.wait_ge(exps_done, 1)
            step_on(reduce(total[:], exps[:], AX, ALU.add))
            step_on(nc.vector.reciprocal(gates[:, 0], total[:]))
            dve.wait_ge(exps_done, 2)
            step_on(tt(gates[:, 1], gates[:, 0], exp_second[:], ALU.mult))
            step_on(ts(gates[:], gates[:], 1.0 - ALPHA, None, ALU.mult))
            unit_lo(0)
            dve.wait_ge(places_done, 1)
            step_on(tt(filled[:], px[:, TT * E:TT * E + E].unsqueeze(2).to_broadcast([P, E, TT]),
                       thresholds[:].unsqueeze(1).to_broadcast([P, E, TT]), ALU.is_gt))
            step_on(reduce(base[:, 0, 4:], filled[:], AX, ALU.add))
            for k, by in enumerate((1, 2, 4)):
                step_on(tt(base[:, k + 1, 4:], base[:, k, 4:], base[:, k, 4 - by:4 - by + E], ALU.add))
            unit_mix(1)
            step_on(stt(place[:], base[:, 3, 3:3 + E].unsqueeze(1).to_broadcast([P, TT, E]), float(P),
                        px[:, 0:TT * E].rearrange("p (j e) -> p j e", e=E), ALU.mult, ALU.add))
            step_on(tt(place_of[:], chosen[:], place[:].unsqueeze(1).to_broadcast([P, TOPK, TT, E]), ALU.mult))
            step_on(reduce(pos_f[:], place_of[:].rearrange("p k j e -> p (k j) e"), AX, ALU.add))
            step_on(nc.vector.tensor_copy(pos[:], pos_f[:]))
            step_on(ts(in_tile[:], pos[:], P - 1, None, ALU.bitwise_and), wait=False)
            step_on(ts(tile_at[:], pos[:], P.bit_length() - 1, None, ALU.logical_shift_right))
            unit_lo(1)
            step_on(tt(hot_tile[:], tile_at[:].unsqueeze(2).to_broadcast([P, PAIRS, NTP]),
                       tile_iota[:].unsqueeze(1).to_broadcast([P, PAIRS, NTP]), ALU.is_equal), wait=False)
            for k in range(TOPK):
                step_on(nc.vector.tensor_copy(payload[:, TT * k:TT * k + TT, 0], token_iota[:]), wait=False)
            flat_gates = gates[:].rearrange("p k j -> p (k j)")
            step_on(nc.vector.tensor_copy(payload[:, :, 1], flat_gates))
            step_on(tt(payload[:, :, 2], flat_gates, payload[:, :, 1].bitcast(F32), ALU.subtract))
            unit_mix(2)
            step_on(tt(spread[:], hot_tile[:].unsqueeze(2).to_broadcast([P, PAIRS, 3, NTP]),
                       payload[:].bitcast(F32).unsqueeze(3).to_broadcast([P, PAIRS, 3, NTP]), ALU.mult), wait=False)
            unit_lo(2)
            for k in range(TOPK):
                tt(hot_slot[:, TT * k:TT * k + TT], in_tile[:, TT * k:TT * k + TT].unsqueeze(2).to_broadcast([P, TT, P]),
                   slot_iota[:].unsqueeze(1).to_broadcast([P, TT, P]), ALU.is_equal).then_inc(hot_done, 1)
                if k == 0:
                    unit_mix(3)
            step_on(tt(passed[:], tile_iota[:].unsqueeze(2).to_broadcast([P, NTP, E]),
                       base[:, 3, 4:].unsqueeze(1).to_broadcast([P, NTP, E]), ALU.is_ge))
            step_on(reduce(expert_of[:], passed[:], AX, ALU.add))
            ts(tile_expert[:], expert_of[:], float(E - 1), None, ALU.min).then_inc(experts_ready, 1)
            unit_lo(3)
            weights_lo(LO_ON_VECTOR[1])
            unit_mix(4)
            dve.wait_ge(dispatched, 1)
            step_on(nc.vector.tensor_copy(slot_info[:], px[:, 0:3 * NTP].rearrange("p (c t) -> p c t", c=3)))
            ts(src_idx[:], slot_info[:, 0], -1.0, 0.0, ALU.add, ALU.max).then_inc(src_ready, 1)
            step_on(tt(slot_gate[:], slot_info[:, 1], slot_info[:, 2], ALU.add), wait=False)
            step_on(ts(empty[:], slot_info[:, 0], 0.0, dump_row[:, 0:1], ALU.is_equal, ALU.mult))
            stt(dst_idx[:], slot_info[:, 0], -1.0, empty[:], ALU.add, ALU.add).then_inc(dst_ready, 1)
            dve.wait_ge(rows_in, 16)
            for u in range(5, UNITS):
                unit_lo(u - 1)
                unit_mix(u)
                if u == FC + 1:
                    shared_out(0)
                if u == FC + 1:
                    weights_lo(LO_ON_VECTOR[2])

            def mix(t, s):
                dve.wait_ge(u_done, UNITS + t + 1)
                dve.wait_ge(silu_done, UNITS + t + 1)
                stt(h[:, s], silu[:, s], slot_gate[:, bass.ds(t, 1)], gu[:, 2 + s], ALU.mult,
                    ALU.mult).then_inc(h_done, 1)

            def split_h(t, s):
                dve.wait_ge(hh_done, UNITS + t + 1)
                tt(hl[:, s], hT[:, s], hh[:, s].bitcast(F32), ALU.subtract).then_inc(hl_done, 1)

            def y_rows(t, s, sent):
                dve.wait_ge(y_main_done, t + 1)
                if sent is not None:
                    dve.wait_ge(scattered[s], 16 * sent)
                tt(y[:, s], y_main[:, s], py[:, D:2 * D], ALU.add).then_inc(y_out, 1)

            unit_lo(UNITS - 1)
            mix(0, 0)
            mix(1, 1)
            shared_out(1)
            split_h(0, 0)
            for t in (2, 3):
                mix(t, t % 2)
                split_h(t - 1, (t - 1) % 2)
                y_rows(t - 2, t % 2, None)

            def step(t, turn, r):
                s = r % 2
                mix(t, s)
                split_h(t - 1, 1 - s)
                y_rows(t - 2, s, RING // 2 * turn + r // 2 - 1)
            tile_loop(dve, 4, NT - 1, step)
            split_h(NT - 1, (NT - 1) % 2)
            for t in (NT - 2, NT - 1):
                y_rows(t, t % 2, t // 2)

        @block.tensor
        def _(pe):
            mm = nc.tensor.matmul
            pe.wait_ge(warm_ready, 1)
            for _ in range(WARM):
                mm(py[:], warm[:, 0:P], warm[:], start=True, stop=True)

            pe.wait_ge(cond_ready, 1)
            for b in range(B):
                i = mm(gu[:, b, 0:MODS], cond_wide[:, b], pr[0:C, AT_MODS:AT_MODS + MODS], start=True, stop=True)
            i.then_inc(mods_done, 1)
            pe.wait_ge(x_in, 16)
            pe.wait_ge(down_ready, 1)
            for b in range(B):
                mm(gu[0:H, 2 + b], w_down[:, b], xT[:, S * b:S * b + S], start=True, stop=True).then_inc(inner_done, 1)
            pe.wait_ge(up_ready, 1)
            for b in range(B):
                pe.wait_ge(relu_done, b + 1)
                mm(hT[:, b], w_up[:, b], inner[:, S * b:S * b + S], start=True, stop=True).then_inc(adapted, 1)
            for j in range(TT):
                pe.wait_ge(x2_done, j // TB + 1)
                i = mm(px[:, E * j:E * j + E], x2T[:, P * j:P * j + P], pr[:, AT_GATE:AT_GATE + E],
                       start=True, stop=True)
            i.then_inc(logits_done, 1)

            def unit1(u):
                b, c, s = u // FC, u % FC, u % 2
                pe.wait_ge(x2l_done, b + 1)
                if u >= 2:
                    pe.wait_ge(h_done, u - 1)
                tokens = slice(S * b, S * b + S)
                for part, done in ((0, g_done), (1, u_done)):
                    cols = slice(F * part + P * c, F * part + P * c + P)
                    acc = gu[:, 2 * part + s]
                    mm(acc, w13_hi[:, SHARED, cols], x2h[:, tokens], start=True, stop=False)
                    mm(acc, w13_hi[:, SHARED, cols], x2l[:, tokens], start=False, stop=False)
                    mm(acc, w13_lo[:, SHARED, cols], x2h[:, tokens], start=False, stop=True).then_inc(done, 1)

            def unit2(u):
                b, c, s = u // FC, u % FC, u % 2
                pe.wait_ge(hl_done, u + 1)
                if u == FC:
                    pe.wait_ge(yT_copied, 1)
                hi, lo = w2_parts[:, SHARED, c, 0], w2_parts[:, SHARED, c, 1]
                mm(hT[:, 0], hi, hh[:, s], start=(c == 0), stop=False)
                mm(hT[:, 0], lo, hh[:, s], start=False, stop=False)
                i = mm(hT[:, 0], hi, hl[:, s], start=False, stop=(c == FC - 1))
                if c == FC - 1:
                    i.then_inc(yT_done, 1)

            def turn_y(b):
                pe.wait_ge(yT_copied, b + 1)
                for j in range(TB):
                    i = nc.tensor.transpose(py[:, P * j:P * j + P], yT[:, P * j:P * j + P], ident[:])
                i.then_inc(y_turned, 1)

            def turn_rows(b):
                pe.wait_ge(x2l_done, b + 1)
                if b:
                    pe.wait_ge(rows_done, b)
                for j in range(TB):
                    for k, part in enumerate((x2h, x2l)):
                        i = nc.tensor.transpose(
                            hT[:, j // 2, 256 * (j % 2) + P * k:256 * (j % 2) + P * k + P].bitcast(F32R),
                            part[:, S * b + P * j:S * b + P * j + P], ident_r[:])
                i.then_inc(rows_turned, 1)

            pe.wait_ge(consts, 1)
            pe.wait_ge(lo_vector, 1)
            pe.wait_ge(raw_free[0], 1)
            turn_rows(0)
            unit1(0)
            turn_rows(1)
            pe.wait_ge(sel_done, 1)
            places = px[:, 0:TT * E].rearrange("p (j e) -> p j e", e=E)
            mm(places, before[:], sel[:], start=True, stop=False)
            for by in range(1, TT):
                mm(places[:, by:], ones[:], sel[:, 0:TT - by], start=False, stop=(by == TT - 1))
            for j in range(TT):
                i = mm(px[:, TT * E:TT * E + E], ones[:], sel[:, j], start=(j == 0), stop=(j == TT - 1))
            i.then_inc(places_done, 1)
            unit1(1)
            pe.wait_ge(rows_done, B)
            unit2(0)
            unit1(2)
            unit2(1)
            unit1(3)
            unit2(2)
            for n in range(PAIRS):
                pe.wait_ge(hot_done, n // TT + 1)
                i = mm(px[:, 0:3 * NTP], hot_slot[:, n], spread[:, n].rearrange("p c t -> p (c t)"),
                       start=(n == 0), stop=(n == PAIRS - 1))
            i.then_inc(dispatched, 1)
            unit1(4)
            unit2(3)
            unit1(5)
            unit2(4)
            turn_y(0)
            unit1(6)
            unit2(5)
            unit1(7)
            unit2(6)

            def transpose_x(t, turn, r):
                pe.wait_ge(gathered[r], 16 * (turn + 1))
                for k in range(2):
                    i = nc.tensor.transpose(px[:, P * k:P * k + P].bitcast(F32R), xg[:, r, P * k:P * k + P], ident_r[:])
                i.then_inc(xT_done, 1)

            def layer1(t, s):
                e = pe.value_load(tile_expert[0:1, bass.ds(t, 1)], min_val=0, max_val=E)
                pe.wait_ge(xs_done, t + 1)
                for part, done in ((0, g_done), (1, u_done)):
                    acc = gu[:, 2 * part + s]
                    cols = slice(part * F, part * F + F)
                    mm(acc, xs[:, s, 0], w13_hi[:, bass.ds(e, 1), cols], start=True, stop=False)
                    mm(acc, xs[:, s, 0], w13_lo[:, bass.ds(e, 1), cols], start=False, stop=False)
                    mm(acc, xs[:, s, 1], w13_hi[:, bass.ds(e, 1), cols], start=False, stop=True).then_inc(done, 1)

            def transpose_h(t, s):
                pe.wait_ge(h_done, UNITS + t + 1)
                for c in range(FC):
                    i = nc.tensor.transpose(hT[:, s, P * c:P * c + P], h[:, s, P * c:P * c + P], ident[:])
                i.then_inc(hT_done, 1)

            def layer2(t, s, first=False):
                e = pe.value_load(tile_expert[0:1, bass.ds(t, 1)], min_val=0, max_val=E)
                pe.wait_ge(hl_done, UNITS + t + 1)
                if first:
                    pe.wait_ge(shared_done, B)
                else:
                    pe.wait_ge(y_out, t)
                for c in range(FC):
                    f = slice(P * c, P * c + P)
                    mm(py[:, 0:2 * D], hh[:, s, f],
                       w2_parts[:, bass.ds(e, 1), c].rearrange("p e k d -> p (e k d)"), start=(c == 0), stop=False)
                    i = mm(py[:, 0:D], hl[:, s, f],
                           w2_parts[:, bass.ds(e, 1), c, 0].rearrange("p e d -> p (e d)"),
                           start=False, stop=(c == FC - 1))
                i.then_inc(y_done, 1)

            pe.wait_ge(src_ready, 1)
            transpose_x(0, 0, 0)
            pe.wait_ge(experts_ready, 1)
            pe.wait_ge(lo_pool, 2 * (E + 1 - len(LO_ON_VECTOR)))
            pe.wait_ge(lo_vector, len(LO_ON_VECTOR))
            pe.wait_ge(raw_free[0], 3)
            pe.wait_ge(h_done, UNITS - 1)
            layer1(0, 0)
            unit2(7)
            transpose_x(1, 0, 1)
            pe.wait_ge(h_done, UNITS)
            layer1(1, 1)
            turn_y(1)
            transpose_x(2, 0, 2)
            transpose_h(0, 0)
            layer1(2, 0)
            transpose_x(3, 0, 3)
            transpose_h(1, 1)
            layer2(0, 0, first=True)

            def step(t, turn, r):
                s = r % 2
                layer1(t, s)
                nxt = (r + 1) % RING
                transpose_x(t + 1, turn + (r + 1) // RING, nxt)
                transpose_h(t - 1, 1 - s)
                layer2(t - 2, s)
            tile_loop(pe, 3, NT - 2, step)
            layer1(NT - 1, (NT - 1) % 2)
            transpose_h(NT - 2, (NT - 2) % 2)
            layer2(NT - 3, (NT - 3) % 2)
            transpose_h(NT - 1, (NT - 1) % 2)
            layer2(NT - 2, (NT - 2) % 2)
            layer2(NT - 1, (NT - 1) % 2)


WARM = 12
STORE_AFTER = 3


def kernel(**inputs):
    import numpy as np
    import concourse.bacc as bacc
    from concourse.bass_utils import run_bass_kernel_spmd

    given = {k: np.asarray(v) for k, v in inputs.items()}
    x = given["x"]
    B, S, D = x.shape
    E, _, F = given["L0_ffn_w1_e"].shape
    w1_s, w3_s, w2_s = (given["L0_ffn_" + n] for n in ("w1_s", "w3_s", "w2_s"))
    w1 = np.concatenate([given["L0_ffn_w1_e"].transpose(1, 0, 2), w1_s.transpose(1, 0, 2).reshape(D, 1, F)], axis=1)
    w3 = np.concatenate([given["L0_ffn_w3_e"].transpose(1, 0, 2), w3_s.transpose(1, 0, 2).reshape(D, 1, F)], axis=1)
    w2 = np.concatenate([given["L0_ffn_w2_e"], w2_s.reshape(1, F, D)], axis=0)
    small = [np.concatenate([given["L0_cond_" + n] for n in ("down_gamma", "down_beta", "up_gamma", "up_beta")], axis=1),
             given["cond_512"].T, given["L0_cond_down_project"], given["L0_cond_up_project"], given["L0_ffn_gate_W"].T]
    params = np.concatenate([np.pad(a, ((0, 128 - a.shape[0]), (0, 0))) for a in small], axis=1)
    laid = {
        "x": x,
        "x_cols": x.reshape(B * S, D).T,
        "params": params,
        "w13": np.concatenate([w1, w3], axis=2),
        "w2": w2.reshape(E + 1, F // 128, 128, D).transpose(2, 0, 1, 3).reshape(128, E + 1, F // 128 * D),
    }
    nc = bacc.Bacc("TRN2", target_bir_lowering=False, num_devices=1)
    arrays, args = {}, []
    for name, a in laid.items():
        a = np.ascontiguousarray(a)
        arrays["in_" + name] = a
        args.append(nc.dram_tensor("in_" + name, a.shape, mybir.dt.from_np(a.dtype), kind="ExternalInput").ap())
    args.append(nc.dram_tensor("out_0", (B * S + 128, D), F32, kind="ExternalOutput").ap())
    build(nc, *args)
    result = run_bass_kernel_spmd(nc, [arrays], core_ids=[0]).results[0]["out_0"]
    return result[:B * S].reshape(B, S, D)
```

```python
from contextlib import ExitStack

import concourse.bass as bass
from concourse import mybir

F32 = mybir.dt.float32
F32R = mybir.dt.float32r
BF16 = mybir.dt.bfloat16
I32 = mybir.dt.int32
U32 = mybir.dt.uint32
ALU = mybir.AluOpType
ACT = mybir.ActivationFunctionType
AX = mybir.AxisListType.X

P = 128
TOPK = 2
RING = 4
AHEAD = 3
RAW = 4


def build(nc, x_cols, params, w13, w2, out, B):
    D, T = x_cols.shape
    S = T // B
    TT = T // P
    TB = S // P
    E = w13.shape[1] - 1
    F = w13.shape[2] // 2
    FC = F // P
    H = 32
    C = 64
    SHARED = E
    UNITS = B * FC
    NT = TOPK * TT + E - 1
    NTP = NT + NT % 2
    PAIRS = TOPK * TT
    ALPHA = 0.5
    GATE_SHARED = ALPHA / E
    MODS = 2 * H + 2 * D
    AT_MODS, AT_COND, AT_DOWN, AT_UP = 0, MODS, MODS + B, MODS + B + H
    AT_GATE = AT_UP + D
    assert D == P and S == F == 512 and UNITS == 8 and NT == 23 and AT_GATE + E == params.shape[1]

    with ExitStack() as ctx:
        def sb(name, shape, dt=F32):
            return ctx.enter_context(nc.sbuf_tensor(name, shape, dt))

        def psum(name, shape, dt=F32):
            return ctx.enter_context(nc.psum_tensor(name, shape, dt))

        def sem(name):
            return ctx.enter_context(nc.semaphore(name))

        x2_rows = nc.dram_tensor("x2_rows", [T, 2 * D], F32R, kind="Internal").ap()
        sum_b = nc.dram_tensor("sum_b", [T + P, D], F32, kind="Internal").ap()
        sums = [out, sum_b]

        raw = sb("raw", [P, RAW, 3 * F])
        w13_hi = sb("w13_hi", [P, E + 1, 2 * F], F32R)
        w13_lo = sb("w13_lo", [P, E + 1, 2 * F], F32R)
        w2_parts = sb("w2_parts", [P, E + 1, FC, 2, D], F32R)
        pr = sb("pr", [P, params.shape[1]])
        xT = sb("xT", [P, T])
        cond_wide = sb("cond_wide", [C, B, P])
        w_down = sb("w_down", [P, B, H])
        w_up = sb("w_up", [H, B, D])
        small = sb("small", [P, T])
        inner = small[0:H]
        yT = small[:, 0:S]
        x2T = sb("x2T", [P, T])
        x2h = sb("x2h", [P, T], F32R)
        x2l = sb("x2l", [P, T], F32R)
        x2_parts = sb("x2_parts", [P, TT, 2, D], F32R)
        ident = sb("ident", [P, P])
        ident_r = sb("ident_r", [P, P], F32R)
        zeros = sb("zeros", [P, D])
        warm = sb("warm", [P, 512], BF16)
        desc = sb("desc", [P, E])
        thresholds = sb("thresholds", [P, TT])
        tile_iota = sb("tile_iota", [P, NTP])
        slot_iota = sb("slot_iota", [P, P])
        token_iota = sb("token_iota", [P, TT])
        dump_row = sb("dump_row", [P, 1])
        before = sb("before", [P, P], BF16)
        ones = sb("ones", [P, P], BF16)
        top = sb("top", [P, TOPK, TT])
        below = sb("below", [P, TOPK, TT, E])
        left = sb("left", [P, TT, E])
        cand = sb("cand", [P, TT, E])
        best = sb("best", [P, TT])
        chosen = sb("chosen", [P, TOPK, TT, E])
        sel = sb("sel", [P, TT, E], BF16)
        exps = sb("exps", [P, TT, E])
        exp_second = sb("exp_second", [P, TT])
        total = sb("total", [P, TT])
        gates = sb("gates", [P, TOPK, TT])
        filled = sb("filled", [P, E, TT])
        base = sb("base", [P, 4, 4 + E])
        place = sb("place", [P, TT, E])
        place_of = sb("place_of", [P, TOPK, TT, E])
        pos_f = sb("pos_f", [P, PAIRS])
        pos = sb("pos", [P, PAIRS], I32)
        in_tile = sb("in_tile", [P, PAIRS], I32)
        tile_at = sb("tile_at", [P, PAIRS], I32)
        hot_slot = x2_parts[:].rearrange("p j k d -> p (j k) d")
        hot_tile = sb("hot_tile", [P, PAIRS, NTP])
        payload = sb("payload", [P, PAIRS, 3], F32R)
        spread = sb("spread", [P, PAIRS, 3, NTP], F32R)
        slot_info = sb("slot_info", [P, 3, NTP])
        passed = sb("passed", [P, NTP, E])
        expert_of = sb("expert_of", [P, NTP])
        empty = sb("empty", [P, NTP])
        src_idx = sb("src_idx", [P, NTP], U32)
        dst_idx = sb("dst_idx", [P, NTP], U32)
        slot_gate = sb("slot_gate", [P, NTP])
        tile_expert = sb("tile_expert", [P, NTP], I32)
        xg = sb("xg", [P, RING, 2 * D], F32R)
        xs = sb("xs", [P, 2, 2, P], F32R)
        silu = sb("silu", [P, 2, F])
        h = sb("h", [P, 2, F])
        hh = sb("hh", [P, 2, F], F32R)
        hl = sb("hl", [P, 2, F], F32R)
        y_main = small[:, S:S + 2 * D].rearrange("p (s d) -> p s d", s=2)
        y = small[:, S + 2 * D:S + 4 * D].rearrange("p (s d) -> p s d", s=2)
        shared_rows = x2T[:].rearrange("p (j d) -> p j d", d=D)

        gu = psum("gu", [P, 4, 512])
        hT = psum("hT", [P, 2, 512])
        y_rows_last = silu[:, (NT - 1) % 2, 0:D]
        y_end = {NT - 2: gu[:, 2 + NT % 2], NT - 1: gu[:, NT % 2]}
        px = psum("px", [P, 512])
        py = psum("py", [P, 512])

        params_in, x_in = sem("params_in"), sem("x_in")
        w13_in = [sem(f"w13_in{r}") for r in range(RAW)]
        w2_in = [sem(f"w2_in{r}") for r in range(RAW)]
        consts, consts_step, warm_ready = sem("consts"), sem("consts_step"), sem("warm_ready")
        hi_done = sem("hi_done")
        lo_vector, lo_pool = sem("lo_vector"), sem("lo_pool")
        cond_ready, mods_done, scaled = sem("cond_ready"), sem("mods_done"), sem("scaled")
        down_ready, up_ready = sem("down_ready"), sem("up_ready")
        inner_done, relu_done, adapted = sem("inner_done"), sem("relu_done"), sem("adapted")
        x2_done, x2h_done, x2l_done = sem("x2_done"), sem("x2h_done"), sem("x2l_done")
        rows_turned, rows_done, x2_stored = sem("rows_turned"), sem("rows_done"), sem("x2_stored")
        step_done, gate_done, slot_done = sem("step_done"), sem("gate_done"), sem("slot_done")
        logits_done, below_done, second_done, exps_done = (
            sem("logits_done"), sem("below_done"), sem("second_done"), sem("exps_done"))
        sel_done, places_done, hot_done, dispatched = (
            sem("sel_done"), sem("places_done"), sem("hot_done"), sem("dispatched"))
        src_ready, dst_ready, experts_ready = sem("src_ready"), sem("dst_ready"), sem("experts_ready")
        g_done, u_done, silu_done, h_done = sem("g_done"), sem("u_done"), sem("silu_done"), sem("h_done")
        hh_done, hl_done = sem("hh_done"), sem("hl_done")
        unit_added = sem("unit_added")
        yT_copied, y_turned, shared_done = sem("yT_copied"), sem("y_turned"), sem("shared_done")
        gathered = [sem(f"gathered{r}") for r in range(RING)]
        scattered = [sem(f"scattered{s}") for s in range(2)]
        xT_done, xs_done, hT_done, y_done, y_main_done, y_out = (
            sem("xT_done"), sem("xs_done"), sem("hT_done"), sem("y_done"), sem("y_main_done"), sem("y_out"))
        sums_set, zeros_set, merged = sem("sums_set"), sem("zeros_set"), sem("merged")

        block = ctx.enter_context(nc.Block())

        def expert_at(n):
            return SHARED if n == 0 else n - 1

        def lo_count(n):
            if n in LO_ON_POOL:
                return lo_pool, 2 * (LO_ON_POOL.index(n) + 1)
            return lo_vector, 2 * sum(m not in LO_ON_POOL for m in range(n + 1))

        def w2_raw(r):
            return raw[:, r, 2 * F:3 * F].rearrange("p (c d) -> p c d", c=FC)

        def tile_loop(eng, first, last, step):
            rounds = (last - first + 1) // RING
            with eng.Fori(0, rounds) as i:
                for k in range(RING):
                    step(RING * i + (first + k), i + (first + k) // RING, (first + k) % RING)
            for t in range(first + RING * rounds, last + 1):
                step(t, t // RING, t % RING)

        @block.sync
        def _(sp):
            sp.dma_start(pr[:], params).then_inc(params_in, 16)
            sp.dma_start(xT[:], x_cols).then_inc(x_in, 16)
            for n in range(E + 1):
                e, r = expert_at(n), n % RAW
                if n >= RAW:
                    split_by, count = lo_count(n - RAW)
                    sp.wait_ge(split_by, count)
                sp.dma_start(raw[:, r, 0:2 * F], w13[:, e]).then_inc(w13_in[r], 16)
                sp.dma_start(raw[:, r, 2 * F:3 * F], w2[:, e]).then_inc(w2_in[r], 16)
                if n == 2:
                    sp.wait_ge(consts, 1)
                    sp.dma_start(out[T:T + P], zeros[:]).then_inc(zeros_set, 16)
                    sp.dma_start(sum_b.rearrange("(a p) d -> p a d", p=P),
                                 zeros[:].unsqueeze(1).to_broadcast([P, TT + 1, D])).then_inc(zeros_set, 16)
                for b in range(B if n == SUMS_AFTER else 0):
                    sp.wait_ge(shared_done, b + 1)
                    sp.dma_start(out[S * b:S * b + S].rearrange("(j p) d -> p j d", p=P),
                                 shared_rows[:, TB * b:TB * b + TB]).then_inc(sums_set, 16)
                for b in range(B if n == STORE_AFTER else 0):
                    sp.wait_ge(rows_done, b + 1)
                    sp.dma_start(x2_rows.rearrange("(j p) d -> p j d", p=P)[:, TB * b:TB * b + TB].bitcast(F32),
                                 x2_parts[:, TB * b:TB * b + TB].rearrange("p j k d -> p j (k d)").bitcast(F32)
                                 ).then_inc(x2_stored, 16)
            sp.wait_ge(sums_set, 16 * B)
            sp.wait_ge(zeros_set, 16 * 2)
            sp.wait_ge(x2_stored, 16 * B)

        @block.gpsimd
        def _(pool):
            nc.gpsimd.memset(warm[:], 0.0).then_inc(warm_ready, 1)
            nc.gpsimd.memset(ident[:], 0.0).then_inc(consts_step, 1)
            nc.gpsimd.memset(before[:], 0.0).then_inc(consts_step, 1)
            nc.gpsimd.memset(ones[:], 1.0).then_inc(consts_step, 1)
            pool.wait_ge(consts_step, 3)
            nc.gpsimd.affine_select(out=ident[:], in_=ident[:], compare_op=ALU.not_equal, fill=1.0,
                                    base=0, pattern=[[-1, P]], channel_multiplier=1).then_inc(consts_step, 1)
            nc.gpsimd.affine_select(out=before[:], in_=before[:], compare_op=ALU.is_ge, fill=1.0,
                                    base=0, pattern=[[-1, P]], channel_multiplier=1).then_inc(consts_step, 1)
            pool.wait_ge(consts_step, 5)
            nc.gpsimd.tensor_copy(ident_r[:], ident[:]).then_inc(consts_step, 1)
            for ap, pattern, start, per_partition in (
                (desc[:], [[-1, E]], E, 0),
                (thresholds[:], [[P, TT]], 0, 0),
                (tile_iota[:], [[1, NTP]], 0, 0),
                (slot_iota[:], [[1, P]], 0, 0),
                (token_iota[:], [[P, TT]], 1, 1),
                (dump_row[:], [[0, 1]], T + 1, 1),
            ):
                nc.gpsimd.iota(ap, pattern=pattern, base=start, channel_multiplier=per_partition,
                               allow_small_or_imprecise_dtypes=True).then_inc(consts_step, 1)
            nc.gpsimd.memset(zeros[:], 0.0).then_inc(consts_step, 1)
            pool.wait_ge(consts_step, 13)
            for k in range(TOPK):
                nc.gpsimd.tensor_copy(payload[:, TT * k:TT * k + TT, 0], token_iota[:]).then_inc(consts_step, 1)
            pool.wait_ge(consts_step, 15)
            nc.gpsimd.memset(thresholds[:, 0:1], -1.0).then_inc(consts, 1)

            def weights_lo(n, part):
                e, r = expert_at(n), n % RAW
                pool.wait_ge(hi_done, 2 * n + part + 1)
                if part == 0:
                    nc.gpsimd.tensor_tensor(w13_lo[:, e], raw[:, r, 0:2 * F], w13_hi[:, e].bitcast(F32),
                                            ALU.subtract).then_inc(lo_pool, 1)
                else:
                    nc.gpsimd.tensor_tensor(w2_parts[:, e, :, 1], w2_raw(r), w2_parts[:, e, :, 0].bitcast(F32),
                                            ALU.subtract).then_inc(lo_pool, 1)

            def unit_lo(u):
                pool.wait_ge(hh_done, u + 1)
                nc.gpsimd.tensor_tensor(hl[:, u % 2], h[:, u % 2], hh[:, u % 2].bitcast(F32),
                                        ALU.subtract).then_inc(hl_done, 1)

            for n in (0, 1):
                weights_lo(n, 0)
                weights_lo(n, 1)
            unit_lo(0)
            unit_lo(1)
            unit_lo(2)
            weights_lo(2, 0)
            unit_lo(3)

            def gather(t):
                if t >= RING:
                    pool.wait_ge(xT_done, t - RING + 1)
                nc.gpsimd.indirect_dma_start(
                    out=xg[:, t % RING], out_offset=None, in_=x2_rows,
                    in_offset=bass.IndirectOffsetOnAxis(ap=src_idx[:, t:t + 1], axis=0),
                ).then_inc(gathered[t % RING], 16)

            def scatter_add(t):
                pool.wait_ge(y_out, t + 1)
                if t >= 2:
                    pool.wait_ge(scattered[t % 2], 16 * (t // 2))
                nc.gpsimd.indirect_dma_start(
                    out=sums[t % 2], out_offset=bass.IndirectOffsetOnAxis(ap=dst_idx[:, t:t + 1], axis=0),
                    in_=y[:, t % 2] if t < NT - 1 else y_rows_last, in_offset=None, compute_op=ALU.add,
                ).then_inc(scattered[t % 2], 16)

            pool.wait_ge(x2_stored, 16 * B)
            pool.wait_ge(src_ready, 1)
            gather(0)
            gather(1)
            weights_lo(2, 1)
            weights_lo(4, 0)
            gather(2)
            gather(3)
            weights_lo(4, 1)
            for t in range(4, RING + AHEAD - 1):
                gather(t)
            weights_lo(6, 0)
            gather(RING + AHEAD - 1)
            weights_lo(6, 1)
            pool.wait_ge(dst_ready, 1)
            pool.wait_ge(zeros_set, 16 * 2)
            pool.wait_ge(sums_set, 16 * B)
            for t in range(NT):
                if t + RING + AHEAD < NT:
                    gather(t + RING + AHEAD)
                scatter_add(t)
            pool.wait_ge(scattered[0], 16 * ((NT + 1) // 2))
            pool.wait_ge(scattered[1], 16 * (NT // 2))
            pool.dma_start(out[0:T], sum_b[0:T], accum_op=ALU.add,
                           max_dma_last_dim=8192).then_inc(merged, 16)
            pool.wait_ge(merged, 16)

        @block.scalar
        def _(act):
            def weights_hi(n, part):
                e, r = expert_at(n), n % RAW
                if part == 0:
                    act.wait_ge(w13_in[r], 16 * (n // RAW + 1))
                    nc.scalar.activation(w13_hi[:, e], raw[:, r, 0:2 * F], ACT.Copy).then_inc(hi_done, 1)
                else:
                    act.wait_ge(w2_in[r], 16 * (n // RAW + 1))
                    nc.scalar.activation(w2_parts[:, e, :, 0], w2_raw(r), ACT.Copy).then_inc(hi_done, 1)

            def silu_g(n, s):
                act.wait_ge(g_done, n + 1)
                nc.scalar.activation(silu[:, s], gu[:, s], ACT.Silu).then_inc(silu_done, 1)

            def rows_out(b):
                act.wait_ge(rows_turned, b + 1)
                nc.scalar.activation(x2_parts[:, TB * b:TB * b + TB].rearrange("p j k d -> p (j k d)"),
                                     hT[:].rearrange("p k c -> p (k c)"), ACT.Copy).then_inc(rows_done, 1)

            def unit_hi(u):
                act.wait_ge(h_done, u + 1)
                if u >= 2:
                    act.wait_ge(unit_added, u - 1)
                nc.scalar.activation(hh[:, u % 2], h[:, u % 2], ACT.Copy).then_inc(hh_done, 1)

            def shared_out(b):
                act.wait_ge(y_turned, b + 1)
                nc.scalar.activation(shared_rows[:, TB * b:TB * b + TB].rearrange("p j d -> p (j d)"), py[:],
                                     ACT.Copy).then_inc(shared_done, 1)

            weights_hi(0, 0)
            weights_hi(0, 1)
            for b in range(B):
                act.wait_ge(x2_done, b + 1)
                nc.scalar.activation(x2h[:, S * b:S * b + S], x2T[:, S * b:S * b + S], ACT.Copy).then_inc(x2h_done, 1)
            weights_hi(1, 0)
            weights_hi(1, 1)
            act.wait_ge(below_done, 1)
            nc.scalar.activation(exps[:], below[:, 0], ACT.Exp).then_inc(exps_done, 1)
            silu_g(0, 0)
            rows_out(0)
            unit_hi(0)
            silu_g(1, 1)
            rows_out(1)
            for u in range(2, UNITS):
                if u < SILU_FIRST_FROM:
                    unit_hi(u - 1)
                    silu_g(u, u % 2)
                else:
                    silu_g(u, u % 2)
                    if u == UNITS - 1:
                        weights_hi(5, 0)
                    unit_hi(u - 1)
                if u in (2, 3, 4):
                    weights_hi(u, 0)
                    weights_hi(u, 1)

            def split_x(t, s):
                act.wait_ge(xT_done, t + 1)
                nc.scalar.activation(xs[:, s].rearrange("p k q -> p (k q)"), px[:, 0:2 * P],
                                     ACT.Copy).then_inc(xs_done, 1)

            def split_h(t, s):
                act.wait_ge(hT_done, t + 1)
                nc.scalar.activation(hh[:, s], hT[:, s], ACT.Copy).then_inc(hh_done, 1)

            def y_first(t, s, acc=py):
                act.wait_ge(y_done, t + 1)
                nc.scalar.activation(y_main[:, s], acc[:, 0:D], ACT.Copy).then_inc(y_main_done, 1)

            split_x(0, 0)
            unit_hi(UNITS - 1)
            shared_out(0)

            def step(t, turn, r):
                s = r % 2
                silu_g(UNITS + t, s)
                split_x(t + 1, 1 - s)
                if not isinstance(t, int) or t >= 1:
                    split_h(t - 1, 1 - s)
                if not isinstance(t, int) or t >= 2:
                    y_first(t - 2, s)
            for t in range(LOOP_FROM):
                step(t, t // RING, t % RING)
                if t == 1:
                    shared_out(1)
                for n, part in HI_AFTER_TILE.get(t, ()):
                    weights_hi(n, part)
            tile_loop(act, LOOP_FROM, NT - 2, step)
            silu_g(UNITS + NT - 1, (NT - 1) % 2)
            split_h(NT - 2, (NT - 2) % 2)
            y_first(NT - 3, (NT - 3) % 2)
            split_h(NT - 1, (NT - 1) % 2)
            y_first(NT - 2, (NT - 2) % 2, y_end[NT - 2])
            y_first(NT - 1, (NT - 1) % 2, y_end[NT - 1])

        @block.vector
        def _(dve):
            tt, ts, stt = nc.vector.tensor_tensor, nc.vector.tensor_scalar, nc.vector.scalar_tensor_tensor
            reduce = nc.vector.tensor_reduce
            steps, gate_steps, slot_steps = [0], [0], [0]

            def gate_step(ins):
                gate_steps[0] += 1
                ins.then_inc(gate_done, 1)

            def slot_step(ins):
                slot_steps[0] += 1
                ins.then_inc(slot_done, 1)

            def step_on(ins, wait=True):
                steps[0] += 1
                ins.then_inc(step_done, 1)
                if wait:
                    dve.wait_ge(step_done, steps[0])

            def wide(a):
                return a.unsqueeze(2).to_broadcast([P, TT, E])

            def weights_lo(n, part):
                e, r = expert_at(n), n % RAW
                dve.wait_ge(hi_done, 2 * n + part + 1)
                if part == 0:
                    tt(w13_lo[:, e], raw[:, r, 0:2 * F], w13_hi[:, e].bitcast(F32), ALU.subtract).then_inc(lo_vector, 1)
                else:
                    tt(w2_parts[:, e, :, 1], w2_raw(r), w2_parts[:, e, :, 0].bitcast(F32),
                       ALU.subtract).then_inc(lo_vector, 1)

            def unit_mix(u):
                dve.wait_ge(u_done, u + 1)
                dve.wait_ge(silu_done, u + 1)
                if u >= 2:
                    dve.wait_ge(hl_done, u - 1)
                stt(h[:, u % 2], silu[:, u % 2], GATE_SHARED, gu[:, 2 + u % 2], ALU.mult, ALU.mult).then_inc(h_done, 1)

            def unit_lo(u):
                dve.wait_ge(hh_done, u + 1)
                dve.wait_ge(hl_done, u)
                tt(hl[:, u % 2], h[:, u % 2], hh[:, u % 2].bitcast(F32), ALU.subtract).then_inc(hl_done, 1)

            def yT_out(b):
                dve.wait_ge(unit_added, FC * (b + 1))
                if b:
                    dve.wait_ge(y_turned, b)
                tt(yT, hT[:, b], xT[:, S * b:S * b + S], ALU.add).then_inc(yT_copied, 1)

            dve.wait_ge(params_in, 16)
            nc.vector.tensor_copy(cond_wide[:], pr[0:C, AT_COND:AT_COND + B].unsqueeze(2).to_broadcast([C, B, P])
                                  ).then_inc(cond_ready, 1)
            dve.wait_ge(mods_done, 1)
            tt(w_down[:], gu[:, 2:4, 0:H], pr[:, AT_DOWN:AT_DOWN + H].unsqueeze(1).to_broadcast([P, B, H]),
               ALU.mult).then_inc(scaled, 1)
            step_on(nc.vector.memset(base[:], 0.0), wait=False)
            dve.wait_ge(scaled, 1)
            tt(w_down[:], w_down[:], gu[:, 2:4, H:2 * H], ALU.add).then_inc(down_ready, 1)
            dve.wait_ge(mods_done, 2)
            tt(w_up[:], gu[0:H, 0:2, 2 * H:2 * H + D], pr[0:H, AT_UP:AT_UP + D].unsqueeze(1).to_broadcast([H, B, D]),
               ALU.mult).then_inc(scaled, 1)
            dve.wait_ge(scaled, 2)
            tt(w_up[:], w_up[:], gu[0:H, 0:2, 2 * H + D:2 * H + 2 * D], ALU.add).then_inc(up_ready, 1)
            for b in range(B):
                dve.wait_ge(inner_done, b + 1)
                ts(inner[:, S * b:S * b + S], gu[0:H, 2 + b], 0.0, None, ALU.max).then_inc(relu_done, 1)
            dve.wait_ge(x_in, 16)
            for b in range(B):
                dve.wait_ge(adapted, b + 1)
                tt(x2T[:, S * b:S * b + S], hT[:, b], xT[:, S * b:S * b + S], ALU.add).then_inc(x2_done, 1)
            for b in range(B):
                dve.wait_ge(x2h_done, b + 1)
                tt(x2l[:, S * b:S * b + S], x2T[:, S * b:S * b + S], x2h[:, S * b:S * b + S].bitcast(F32),
                   ALU.subtract).then_inc(x2l_done, 1)

            dve.wait_ge(consts, 1)
            desc_w = desc[:].unsqueeze(1).to_broadcast([P, TT, E])

            def pick(k, logits, signal):
                step_on(reduce(top[:, k], logits, AX, ALU.max))
                tt(below[:, k], logits, wide(top[:, k]), ALU.subtract).then_inc(signal, 1)
                dve.wait_ge(signal, 1)
                step_on(stt(cand[:], below[:, k], 0.0, desc_w, ALU.is_equal, ALU.mult))
                step_on(reduce(best[:], cand[:], AX, ALU.max))
                step_on(tt(chosen[:, k], cand[:], wide(best[:]), ALU.is_equal))

            dve.wait_ge(logits_done, 1)
            pick(0, px[:, 0:TT * E].rearrange("p (j e) -> p j e", e=E), below_done)
            step_on(stt(left[:], chosen[:, 0], -1e30, below[:, 0], ALU.mult, ALU.add))
            pick(1, left[:], second_done)
            tt(sel[:], chosen[:, 0], chosen[:, 1], ALU.add).then_inc(sel_done, 1)
            unit_mix(0)
            dve.wait_ge(exps_done, 1)
            gate_step(reduce(total[:], exps[:], AX, ALU.add))
            gate_step(tt(left[:], exps[:], chosen[:, 1], ALU.mult))
            dve.wait_ge(places_done, 1)
            slot_step(tt(filled[:], px[:, TT * E:TT * E + E].unsqueeze(2).to_broadcast([P, E, TT]),
                         thresholds[:].unsqueeze(1).to_broadcast([P, E, TT]), ALU.is_gt))
            dve.wait_ge(gate_done, gate_steps[0])
            gate_step(nc.vector.reciprocal(total[:], total[:]))
            gate_step(reduce(exp_second[:], left[:], AX, ALU.add))
            dve.wait_ge(slot_done, slot_steps[0])
            slot_step(reduce(base[:, 0, 4:], filled[:], AX, ALU.add))
            dve.wait_ge(gate_done, gate_steps[0])
            gate_step(ts(gates[:, 0], total[:], 1.0 - ALPHA, None, ALU.mult))
            dve.wait_ge(slot_done, slot_steps[0])
            slot_step(tt(base[:, 1, 4:], base[:, 0, 4:], base[:, 0, 3:3 + E], ALU.add))
            gate_step(stt(gates[:, 1], total[:], 1.0 - ALPHA, exp_second[:], ALU.mult, ALU.mult))
            dve.wait_ge(slot_done, slot_steps[0])
            slot_step(tt(base[:, 2, 4:], base[:, 1, 4:], base[:, 1, 2:2 + E], ALU.add))
            dve.wait_ge(gate_done, gate_steps[0])
            flat_gates = gates[:].rearrange("p k j -> p (k j)")
            gate_step(nc.vector.tensor_copy(payload[:, :, 1], flat_gates))
            dve.wait_ge(slot_done, slot_steps[0])
            slot_step(tt(base[:, 3, 4:], base[:, 2, 4:], base[:, 2, 0:E], ALU.add))
            dve.wait_ge(gate_done, gate_steps[0])
            gate_step(tt(payload[:, :, 2], flat_gates, payload[:, :, 1].bitcast(F32), ALU.subtract))
            dve.wait_ge(slot_done, slot_steps[0])
            slot_step(stt(place[:], base[:, 3, 3:3 + E].unsqueeze(1).to_broadcast([P, TT, E]), float(P),
                          px[:, 0:TT * E].rearrange("p (j e) -> p j e", e=E), ALU.mult, ALU.add))
            unit_mix(1)
            dve.wait_ge(slot_done, slot_steps[0])
            slot_step(tt(place_of[:], chosen[:], place[:].unsqueeze(1).to_broadcast([P, TOPK, TT, E]), ALU.mult))
            dve.wait_ge(slot_done, slot_steps[0])
            slot_step(reduce(pos_f[:], place_of[:].rearrange("p k j e -> p (k j) e"), AX, ALU.add))
            dve.wait_ge(slot_done, slot_steps[0])
            slot_step(nc.vector.tensor_copy(pos[:], pos_f[:]))
            dve.wait_ge(slot_done, slot_steps[0])
            slot_step(ts(tile_at[:], pos[:], P.bit_length() - 1, None, ALU.logical_shift_right))
            slot_step(ts(in_tile[:], pos[:], P - 1, None, ALU.bitwise_and))
            dve.wait_ge(slot_done, slot_steps[0])
            slot_step(tt(hot_tile[:], tile_at[:].unsqueeze(2).to_broadcast([P, PAIRS, NTP]),
                         tile_iota[:].unsqueeze(1).to_broadcast([P, PAIRS, NTP]), ALU.is_equal))
            unit_mix(2)
            dve.wait_ge(gate_done, gate_steps[0])
            dve.wait_ge(slot_done, slot_steps[0])
            slot_step(tt(spread[:], hot_tile[:].unsqueeze(2).to_broadcast([P, PAIRS, 3, NTP]),
                         payload[:].bitcast(F32).unsqueeze(3).to_broadcast([P, PAIRS, 3, NTP]), ALU.mult))
            dve.wait_ge(x2_stored, 16 * B)
            for k in range(TOPK):
                tt(hot_slot[:, TT * k:TT * k + TT], in_tile[:, TT * k:TT * k + TT].unsqueeze(2).to_broadcast([P, TT, P]),
                   slot_iota[:].unsqueeze(1).to_broadcast([P, TT, P]), ALU.is_equal).then_inc(hot_done, 1)
                if k == 0:
                    unit_mix(3)
            step_on(tt(passed[:], tile_iota[:].unsqueeze(2).to_broadcast([P, NTP, E]),
                       base[:, 3, 4:].unsqueeze(1).to_broadcast([P, NTP, E]), ALU.is_ge))
            step_on(reduce(expert_of[:], passed[:], AX, ALU.add))
            ts(tile_expert[:], expert_of[:], float(E - 1), None, ALU.min).then_inc(experts_ready, 1)
            unit_mix(4)
            dve.wait_ge(dispatched, 1)
            step_on(nc.vector.tensor_copy(slot_info[:], px[:, 0:3 * NTP].rearrange("p (c t) -> p c t", c=3)))
            ts(src_idx[:], slot_info[:, 0], -1.0, 0.0, ALU.add, ALU.max).then_inc(src_ready, 1)
            step_on(tt(slot_gate[:], slot_info[:, 1], slot_info[:, 2], ALU.add), wait=False)
            step_on(ts(empty[:], slot_info[:, 0], 0.0, dump_row[:, 0:1], ALU.is_equal, ALU.mult))
            stt(dst_idx[:], slot_info[:, 0], -1.0, empty[:], ALU.add, ALU.add).then_inc(dst_ready, 1)
            for u in range(5, UNITS):
                unit_mix(u)
                unit_lo(u - 1)
                if u == YT_AFTER:
                    yT_out(0)
            unit_lo(UNITS - 1)

            def mix(t, s):
                dve.wait_ge(u_done, UNITS + t + 1)
                dve.wait_ge(silu_done, UNITS + t + 1)
                stt(h[:, s], silu[:, s], slot_gate[:, bass.ds(t, 1)], gu[:, 2 + s], ALU.mult,
                    ALU.mult).then_inc(h_done, 1)

            def split_h(t, s):
                dve.wait_ge(hh_done, UNITS + t + 1)
                tt(hl[:, s], hT[:, s], hh[:, s].bitcast(F32), ALU.subtract).then_inc(hl_done, 1)

            def y_rows(t, s, sent, acc=py, rows=None):
                dve.wait_ge(y_main_done, t + 1)
                if sent is not None:
                    dve.wait_ge(scattered[s], 16 * sent)
                tt(y[:, s] if rows is None else rows, y_main[:, s], acc[:, D:2 * D], ALU.add).then_inc(y_out, 1)

            def step(t, turn, r):
                s = r % 2
                mix(t, s)
                if not isinstance(t, int) or t >= 1:
                    split_h(t - 1, 1 - s)
                if not isinstance(t, int) or t >= 4:
                    y_rows(t - 2, s, RING // 2 * turn + r // 2 - 1)
                elif t >= 2:
                    y_rows(t - 2, s, None)
            for t in range(LOOP_FROM):
                step(t, t // RING, t % RING)
                for n, part in LO_AFTER_TILE.get(t, ()):
                    weights_lo(n, part)
                if t == 0:
                    yT_out(1)
            tile_loop(dve, LOOP_FROM, NT - 1, step)
            split_h(NT - 1, (NT - 1) % 2)
            y_rows(NT - 2, (NT - 2) % 2, (NT - 2) // 2, y_end[NT - 2])
            y_rows(NT - 1, (NT - 1) % 2, None, y_end[NT - 1], y_rows_last)

        @block.tensor
        def _(pe):
            mm = nc.tensor.matmul

            def busy(count):
                for _ in range(count):
                    mm(py[:], warm[:, 0:P], warm[:], start=True, stop=True)

            pe.wait_ge(warm_ready, 1)
            busy(WARM)

            pe.wait_ge(cond_ready, 1)
            for bank, part in ((2, slice(0, 2 * H)), (0, slice(2 * H, MODS))):
                for b in range(B):
                    i = mm(gu[:, bank + b, part], cond_wide[:, b], pr[0:C, part], start=True, stop=True)
                i.then_inc(mods_done, 1)
                busy(WARM_MODS)
            pe.wait_ge(x_in, 16)
            pe.wait_ge(down_ready, 1)
            for b in range(B):
                mm(gu[0:H, 2 + b], w_down[:, b], xT[:, S * b:S * b + S], start=True, stop=True).then_inc(inner_done, 1)
            pe.wait_ge(up_ready, 1)
            for b in range(B):
                pe.wait_ge(relu_done, b + 1)
                mm(hT[:, b], w_up[:, b], inner[:, S * b:S * b + S], start=True, stop=True).then_inc(adapted, 1)
            for j in range(TT):
                if j % TB == 0:
                    busy(WARM_LOGITS)
                pe.wait_ge(x2_done, j // TB + 1)
                i = mm(px[:, E * j:E * j + E], x2T[:, P * j:P * j + P], pr[:, AT_GATE:AT_GATE + E],
                       start=True, stop=True)
            i.then_inc(logits_done, 1)

            def unit1(u):
                b, c, s = u // FC, u % FC, u % 2
                pe.wait_ge(x2l_done, b + 1)
                if u >= 2:
                    pe.wait_ge(h_done, u - 1)
                tokens = slice(S * b, S * b + S)
                for part, done in ((0, g_done), (1, u_done)):
                    cols = slice(F * part + P * c, F * part + P * c + P)
                    acc = gu[:, 2 * part + s]
                    mm(acc, w13_hi[:, SHARED, cols], x2h[:, tokens], start=True, stop=False)
                    mm(acc, w13_hi[:, SHARED, cols], x2l[:, tokens], start=False, stop=False)
                    mm(acc, w13_lo[:, SHARED, cols], x2h[:, tokens], start=False, stop=True).then_inc(done, 1)

            def unit2(u):
                b, c, s = u // FC, u % FC, u % 2
                pe.wait_ge(hl_done, u + 1)
                hi, lo = w2_parts[:, SHARED, c, 0], w2_parts[:, SHARED, c, 1]
                mm(hT[:, b], hi, hh[:, s], start=(c == 0), stop=False)
                mm(hT[:, b], lo, hh[:, s], start=False, stop=False)
                mm(hT[:, b], hi, hl[:, s], start=False, stop=(c == FC - 1)).then_inc(unit_added, 1)

            def turn_y(b):
                pe.wait_ge(yT_copied, b + 1)
                if b:
                    pe.wait_ge(shared_done, b)
                for j in range(TB):
                    i = nc.tensor.transpose(py[:, P * j:P * j + P], yT[:, P * j:P * j + P], ident[:])
                i.then_inc(y_turned, 1)

            def turn_rows(b):
                pe.wait_ge(x2l_done, b + 1)
                if b:
                    pe.wait_ge(rows_done, b)
                for j in range(TB):
                    for k, part in enumerate((x2h, x2l)):
                        i = nc.tensor.transpose(
                            hT[:, j // 2, 256 * (j % 2) + P * k:256 * (j % 2) + P * k + P].bitcast(F32R),
                            part[:, S * b + P * j:S * b + P * j + P], ident_r[:])
                i.then_inc(rows_turned, 1)

            pe.wait_ge(consts, 1)
            split_by, count = lo_count(0)
            pe.wait_ge(split_by, count)
            turn_rows(0)
            unit1(0)
            pe.wait_ge(sel_done, 1)
            places = px[:, 0:TT * E].rearrange("p (j e) -> p j e", e=E)
            mm(places, before[:], sel[:], start=True, stop=False)
            for by in range(1, TT):
                mm(places[:, by:], ones[:], sel[:, 0:TT - by], start=False, stop=(by == TT - 1))
            for j in range(TT):
                i = mm(px[:, TT * E:TT * E + E], ones[:], sel[:, j], start=(j == 0), stop=(j == TT - 1))
            i.then_inc(places_done, 1)
            turn_rows(1)
            unit1(1)
            unit1(2)
            pe.wait_ge(rows_done, B)
            unit2(0)
            unit1(3)
            unit2(1)
            unit1(4)
            unit2(2)
            for n in range(PAIRS):
                pe.wait_ge(hot_done, n // TT + 1)
                i = mm(px[:, 0:3 * NTP], hot_slot[:, n], spread[:, n].rearrange("p c t -> p (c t)"),
                       start=(n == 0), stop=(n == PAIRS - 1))
                if n == TT - 1:
                    unit1(5)
            i.then_inc(dispatched, 1)
            unit2(3)
            unit1(6)
            unit1(7)
            unit2(4)

            def transpose_x(t, turn, r):
                pe.wait_ge(gathered[r], 16 * (turn + 1))
                for k in range(2):
                    i = nc.tensor.transpose(px[:, P * k:P * k + P].bitcast(F32R), xg[:, r, P * k:P * k + P], ident_r[:])
                i.then_inc(xT_done, 1)

            expert = [pe.alloc_register(f"expert{r}") for r in range(RING)]

            def load_expert(t, r):
                pe.reg_load(expert[r], tile_expert[0:1, bass.ds(t, 1)])

            def layer1(t, r, load=True):
                e, s = pe.snap(expert[r], min_val=0, max_val=E), r % 2
                pe.wait_ge(xs_done, t + 1)
                for part, done in ((0, g_done), (1, u_done)):
                    if part and load:
                        load_expert(t + 1, (r + 1) % RING)
                    acc = gu[:, 2 * part + s]
                    cols = slice(part * F, part * F + F)
                    mm(acc, xs[:, s, 0], w13_hi[:, bass.ds(e, 1), cols], start=True, stop=False)
                    mm(acc, xs[:, s, 0], w13_lo[:, bass.ds(e, 1), cols], start=False, stop=False)
                    mm(acc, xs[:, s, 1], w13_hi[:, bass.ds(e, 1), cols], start=False, stop=True).then_inc(done, 1)

            def transpose_h(t, s):
                pe.wait_ge(h_done, UNITS + t + 1)
                for c in range(FC):
                    i = nc.tensor.transpose(hT[:, s, P * c:P * c + P], h[:, s, P * c:P * c + P], ident[:])
                i.then_inc(hT_done, 1)

            def layer2(t, r, first=False, acc=py):
                e, s = pe.snap(expert[r], min_val=0, max_val=E), r % 2
                pe.wait_ge(hl_done, UNITS + t + 1)
                if first:
                    pe.wait_ge(shared_done, B)
                elif acc is py:
                    pe.wait_ge(y_out, t)
                for c in range(FC):
                    f = slice(P * c, P * c + P)
                    mm(acc[:, 0:2 * D], hh[:, s, f],
                       w2_parts[:, bass.ds(e, 1), c].rearrange("p e k d -> p (e k d)"), start=(c == 0), stop=False)
                    i = mm(acc[:, 0:D], hl[:, s, f],
                           w2_parts[:, bass.ds(e, 1), c, 0].rearrange("p e d -> p (e d)"),
                           start=False, stop=(c == FC - 1))
                i.then_inc(y_done, 1)

            def step(t, turn, r):
                layer1(t, r)
                if not isinstance(t, int) or t >= 1:
                    transpose_x(t + 1, turn + (r + 1) // RING, (r + 1) % RING)
                    transpose_h(t - 1, (r + 1) % 2)
                if not isinstance(t, int) or t >= 2:
                    layer2(t - 2, (r + 2) % RING, first=isinstance(t, int) and t == 2)

            pe.wait_ge(src_ready, 1)
            transpose_x(0, 0, 0)
            unit2(5)
            turn_y(0)
            pe.wait_ge(experts_ready, 1)
            load_expert(0, 0)
            pe.wait_ge(h_done, UNITS - 1)
            for t in range(LOOP_FROM):
                split_by, count = lo_count(t)
                pe.wait_ge(split_by, count)
                split_by, count = lo_count(t + 1)
                pe.wait_ge(split_by, count - 1)
                step(t, t // RING, t % RING)
                if t == 0:
                    transpose_x(1, 0, 1)
                    unit2(UNITS - 2)
                    unit2(UNITS - 1)
                    pe.wait_ge(h_done, UNITS)
                if t == 1:
                    turn_y(1)
            split_by, count = lo_count(E)
            pe.wait_ge(split_by, count)
            tile_loop(pe, LOOP_FROM, NT - 2, step)
            layer1(NT - 1, (NT - 1) % RING, load=False)
            transpose_h(NT - 2, (NT - 2) % 2)
            layer2(NT - 3, (NT - 3) % RING)
            transpose_h(NT - 1, (NT - 1) % 2)
            layer2(NT - 2, (NT - 2) % RING, acc=y_end[NT - 2])
            layer2(NT - 1, (NT - 1) % RING, acc=y_end[NT - 1])


WARM, WARM_MODS, WARM_LOGITS = 9, 1, 1
STORE_AFTER, SUMS_AFTER = 4, 7
YT_AFTER = 6
SILU_FIRST_FROM = 6
LOOP_FROM = 8
LO_ON_POOL = (0, 1, 2, 4, 6)
HI_AFTER_TILE = {0: ((5, 1), (6, 0)), 1: ((6, 1),), 2: ((7, 0),), 3: ((7, 1),), 4: ((8, 0),), 5: ((8, 1),)}
LO_AFTER_TILE = {0: ((3, 0), (3, 1)), 1: ((5, 0),), 2: ((5, 1),), 3: ((7, 0),), 4: ((7, 1),), 5: ((8, 0),), 6: ((8, 1),)}


def kernel(**inputs):
    import numpy as np
    import concourse.bacc as bacc
    from concourse.bass_utils import run_bass_kernel_spmd

    given = {k: np.asarray(v) for k, v in inputs.items()}
    x = given["x"]
    B, S, D = x.shape
    E, _, F = given["L0_ffn_w1_e"].shape
    w1_s, w3_s, w2_s = (given["L0_ffn_" + n] for n in ("w1_s", "w3_s", "w2_s"))
    w1 = np.concatenate([given["L0_ffn_w1_e"].transpose(1, 0, 2), w1_s.transpose(1, 0, 2).reshape(D, 1, F)], axis=1)
    w3 = np.concatenate([given["L0_ffn_w3_e"].transpose(1, 0, 2), w3_s.transpose(1, 0, 2).reshape(D, 1, F)], axis=1)
    w2 = np.concatenate([given["L0_ffn_w2_e"], w2_s.reshape(1, F, D)], axis=0)
    small = [np.concatenate([given["L0_cond_" + n] for n in ("down_gamma", "down_beta", "up_gamma", "up_beta")], axis=1),
             given["cond_512"].T, given["L0_cond_down_project"], given["L0_cond_up_project"], given["L0_ffn_gate_W"].T]
    params = np.concatenate([np.pad(a, ((0, 128 - a.shape[0]), (0, 0))) for a in small], axis=1)
    laid = {
        "x_cols": x.reshape(B * S, D).T,
        "params": params,
        "w13": np.concatenate([w1, w3], axis=2),
        "w2": w2.reshape(E + 1, F // 128, 128, D).transpose(2, 0, 1, 3).reshape(128, E + 1, F // 128 * D),
    }
    nc = bacc.Bacc("TRN2", target_bir_lowering=False, num_devices=1)
    arrays, args = {}, []
    for name, a in laid.items():
        a = np.ascontiguousarray(a)
        arrays["in_" + name] = a
        args.append(nc.dram_tensor("in_" + name, a.shape, mybir.dt.from_np(a.dtype), kind="ExternalInput").ap())
    args.append(nc.dram_tensor("out_0", (B * S + 128, D), F32, kind="ExternalOutput").ap())
    build(nc, *args, B)
    result = run_bass_kernel_spmd(nc, [arrays], core_ids=[0]).results[0]["out_0"]
    return result[:B * S].reshape(B, S, D)
```
